# Optimizing a Trainium2 kernel written in Bass

```python
import numpy as np
import jax
import jax.numpy as jnp

def _softmax(x, axis=-1):
    return jax.nn.softmax(x, axis=axis)

def _gelu(x):
    return jax.nn.gelu(x, approximate=True)

def _silu(x):
    return jax.nn.silu(x)

def _sigmoid(x):
    return jax.nn.sigmoid(x)

def _layernorm(x, axis=-1, eps=1e-05):
    m = jnp.mean(x, axis=axis, keepdims=True)
    v = jnp.var(x, axis=axis, keepdims=True)
    return (x - m) / jnp.sqrt(v + eps)

def _scatter_add(tgt, idx, src, axis=0):
    return tgt.at[idx].add(src)

def _segment_sum(src, seg, n):
    return jax.ops.segment_sum(src, seg, n)
kernel_name = 'mk_perceiver_d1_seqx_r4_83832b'

def setup_inputs(seed: int=0):
    np.random.seed(seed)
    _w = jnp.asarray

    def _rec_inputs():
        import jax
        import jax.numpy as jnp
        _rk = jax.random.key(seed)
        x = -0.0003929 + 0.9999 * jax.random.normal(jax.random.fold_in(_rk, 1), (1, 256, 256), jnp.float32)
        _lenS = 256 - jax.random.randint(jax.random.fold_in(_rk, 7), (1,), 0, max(1, 256 // 4) + 1, jnp.int32)
        _lenS2 = 4096 - jax.random.randint(jax.random.fold_in(_rk, 8), (1,), 0, max(1, 4096 // 4) + 1, jnp.int32)
        _ctx_1024P = jax.random.normal(jax.random.fold_in(_rk, 11), (1, 16, 256), jnp.float32)
        _ctx_1024c = jax.random.dirichlet(jax.random.fold_in(_rk, 511), 0.3 * jnp.ones((16,), jnp.float32), (1, 4096))
        _ctx_1024t = jnp.einsum('bsk,bkd->bsd', _ctx_1024c, _ctx_1024P)
        _ctx_1024t = _ctx_1024t * jax.lax.rsqrt(jnp.mean(jnp.square(_ctx_1024t)) + 1e-12) * 0.953939
        ctx_1024 = 2.81802e-05 + 1.00001 * (_ctx_1024t + 0.3 * jax.random.normal(jax.random.fold_in(_rk, 611), (1, 4096, 256), jnp.float32))
        return (x, ctx_1024)
    x, ctx_1024 = _rec_inputs()

    def _L0_xattn_setup():
        import jax, jax.numpy as jnp
        import numpy as np
        EMBED = 256
        B, I, J = (8, 512, 512)
        SCALE = EMBED ** (-0.5)
        key = jax.random.key(seed)
        ks = jax.random.split(key, 5)
        s = EMBED ** (-0.5)
        return {'q_in': jax.random.normal(ks[0], (B, I, EMBED), dtype=jnp.float32), 'k_v': jax.random.normal(ks[1], (B, J, EMBED), dtype=jnp.float32), 'Wq': jax.random.normal(ks[2], (EMBED, EMBED), dtype=jnp.float32) * s, 'bq': jnp.zeros((EMBED,), dtype=jnp.float32), 'Wk': jax.random.normal(ks[3], (EMBED, EMBED), dtype=jnp.float32) * s, 'bk': jnp.zeros((EMBED,), dtype=jnp.float32), 'Wv': jax.random.normal(ks[4], (EMBED, EMBED), dtype=jnp.float32) * s, 'bv': jnp.zeros((EMBED,), dtype=jnp.float32)}
    _L0_xattn_all = _L0_xattn_setup()
    _L0_xattn_in = {k: v for k, v in _L0_xattn_all.items() if k in ('Wq', 'bq', 'Wk', 'bk', 'Wv', 'bv')}
    del _L0_xattn_all

    def _L0_attn_setup():
        import jax, jax.numpy as jnp
        import numpy as np
        B, T, C = (4, 1024, 256)
        H = 16
        LS = 64
        EPS = 1e-06

        def rmsnorm(x, w):
            xf = x.astype(jnp.float32)
            y = xf * jax.lax.rsqrt(jnp.mean(xf * xf, axis=-1, keepdims=True) + EPS)
            return y.astype(x.dtype) * w
        key = jax.random.key(seed)
        k1, k2, k3 = jax.random.split(key, 3)
        x = jax.random.normal(k1, (B, T, C), dtype=jnp.float32)
        w_qkv = jax.random.normal(k2, (C, 3 * C), dtype=jnp.float32) * (1.0 / np.sqrt(C))
        ln_w = jnp.ones((C,), dtype=jnp.float32)
        w_proj = jax.random.normal(k3, (C, C), dtype=jnp.float32) * (1.0 / np.sqrt(C))
        return {'x': x, 'w_qkv': w_qkv, 'ln_w': ln_w, 'w_proj': w_proj}
    _L0_attn_all = _L0_attn_setup()
    _L0_attn_in = {k: v for k, v in _L0_attn_all.items() if k in ('w_qkv', 'ln_w', 'w_proj')}
    del _L0_attn_all

    def _L0_ffn_setup():
        import jax, jax.numpy as jnp
        import numpy as np
        MICRO_BATCHES = 2
        TOP_K = 2
        LN_EPS = 1e-05
        B, S, D = (4, 1024, 256)
        E = 8
        DFF = 4 * D

        def _layernorm(x, g, b):
            mu = jnp.mean(x, axis=-1, keepdims=True)
            var = jnp.mean(jnp.square(x - mu), axis=-1, keepdims=True)
            return (x - mu) * jax.lax.rsqrt(var + LN_EPS) * g + b
        key = jax.random.key(seed)
        ks = jax.random.split(key, 12)
        sd = 1.0 / np.sqrt(D)
        sf = 1.0 / np.sqrt(DFF)
        return {'x': jax.random.normal(ks[0], (B, S, D), dtype=jnp.float32), 'ln_g': jnp.ones((D,), jnp.float32), 'ln_b': jnp.zeros((D,), jnp.float32), 'attn_w': jax.random.normal(ks[1], (D, D), jnp.float32) * sd, 'attn_b': jnp.zeros((D,), jnp.float32), 'gate_w': jax.random.normal(ks[2], (D, E), jnp.float32) * sd, 'w1': jax.random.normal(ks[3], (E, D, DFF), jnp.float32) * sd, 'b1': jnp.zeros((E, DFF), jnp.float32), 'w2': jax.random.normal(ks[4], (E, DFF, D), jnp.float32) * sf, 'b2': jnp.zeros((E, D), jnp.float32), 'next_w': jax.random.normal(ks[5], (D, D), jnp.float32) * sd, 'next_b': jnp.zeros((D,), jnp.float32)}
    _L0_ffn_all = _L0_ffn_setup()
    _L0_ffn_in = {k: v for k, v in _L0_ffn_all.items() if k in ('ln_g', 'ln_b', 'attn_w', 'attn_b', 'gate_w', 'w1', 'b1', 'w2', 'b2', 'next_w', 'next_b')}
    del _L0_ffn_all
    return {'x': x, 'ctx_1024': ctx_1024, 'L0_xattn_Wq': _L0_xattn_in['Wq'], 'L0_xattn_bq': _L0_xattn_in['bq'], 'L0_xattn_Wk': _L0_xattn_in['Wk'], 'L0_xattn_bk': _L0_xattn_in['bk'], 'L0_xattn_Wv': _L0_xattn_in['Wv'], 'L0_xattn_bv': _L0_xattn_in['bv'], 'L0_attn_w_qkv': _L0_attn_in['w_qkv'], 'L0_attn_ln_w': _L0_attn_in['ln_w'], 'L0_attn_w_proj': _L0_attn_in['w_proj'], 'L0_ffn_ln_g': _L0_ffn_in['ln_g'], 'L0_ffn_ln_b': _L0_ffn_in['ln_b'], 'L0_ffn_attn_w': _L0_ffn_in['attn_w'], 'L0_ffn_attn_b': _L0_ffn_in['attn_b'], 'L0_ffn_gate_w': _L0_ffn_in['gate_w'], 'L0_ffn_w1': _L0_ffn_in['w1'], 'L0_ffn_b1': _L0_ffn_in['b1'], 'L0_ffn_w2': _L0_ffn_in['w2'], 'L0_ffn_b2': _L0_ffn_in['b2'], 'L0_ffn_next_w': _L0_ffn_in['next_w'], 'L0_ffn_next_b': _L0_ffn_in['next_b']}

def reference(x, ctx_1024, L0_xattn_Wq, L0_xattn_bq, L0_xattn_Wk, L0_xattn_bk, L0_xattn_Wv, L0_xattn_bv, L0_attn_w_qkv, L0_attn_ln_w, L0_attn_w_proj, L0_ffn_ln_g, L0_ffn_ln_b, L0_ffn_attn_w, L0_ffn_attn_b, L0_ffn_gate_w, L0_ffn_w1, L0_ffn_b1, L0_ffn_w2, L0_ffn_b2, L0_ffn_next_w, L0_ffn_next_b):
    import jax
    import jax.numpy as jnp

    def _L0_xattn_ref(q_in, k_v, Wq, bq, Wk, bk, Wv, bv):
        import jax, jax.numpy as jnp
        import numpy as np
        EMBED = 256
        B, I, J = (8, 512, 512)
        SCALE = EMBED ** (-0.5)
        q = q_in @ Wq + bq
        k = k_v @ Wk + bk
        v = k_v @ Wv + bv
        sim = jnp.einsum('bid,bjd->bij', q, k) * SCALE
        attn = jax.nn.softmax(sim, axis=-1)
        out = jnp.einsum('bij,bjd->bid', attn, v)
        return out

    def _L0_attn_ref(x, w_qkv, ln_w, w_proj):
        import jax, jax.numpy as jnp
        import numpy as np
        B, T, C = (4, 1024, 256)
        H = 16
        LS = 64
        EPS = 1e-06

        def rmsnorm(x, w):
            xf = x.astype(jnp.float32)
            y = xf * jax.lax.rsqrt(jnp.mean(xf * xf, axis=-1, keepdims=True) + EPS)
            return y.astype(x.dtype) * w
        Bx, Tx, Cx = x.shape
        ng = Tx // LS
        hd = Cx // H
        xg = x.reshape(Bx, ng, LS, Cx)
        qkv = jnp.einsum('bglc,cd->bgld', xg, w_qkv)
        q, k, v = jnp.split(qkv, 3, axis=-1)
        q = rmsnorm(q, ln_w)
        k = rmsnorm(k, ln_w)
        q = q.reshape(Bx, ng, LS, H, hd).transpose(0, 1, 3, 2, 4)
        k = k.reshape(Bx, ng, LS, H, hd).transpose(0, 1, 3, 2, 4)
        v = v.reshape(Bx, ng, LS, H, hd).transpose(0, 1, 3, 2, 4)
        scale = 1.0 / np.sqrt(hd)
        att = jnp.einsum('bghqd,bghkd->bghqk', q, k) * scale
        causal = jnp.tril(jnp.ones((LS, LS), dtype=bool))
        att = jnp.where(causal, att, -jnp.finfo(att.dtype).max)
        att = jax.nn.softmax(att, axis=-1)
        y = jnp.einsum('bghqk,bghkd->bghqd', att, v)
        y = y.transpose(0, 1, 3, 2, 4).reshape(Bx, Tx, Cx)
        return jnp.einsum('btc,cd->btd', y, w_proj)

    def _L0_ffn_ref(x, ln_g, ln_b, attn_w, attn_b, gate_w, w1, b1, w2, b2, next_w, next_b):
        import jax, jax.numpy as jnp
        import numpy as np
        MICRO_BATCHES = 2
        TOP_K = 2
        LN_EPS = 1e-05
        B, S, D = (4, 1024, 256)
        E = 8
        DFF = 4 * D

        def _layernorm(x, g, b):
            mu = jnp.mean(x, axis=-1, keepdims=True)
            var = jnp.mean(jnp.square(x - mu), axis=-1, keepdims=True)
            return (x - mu) * jax.lax.rsqrt(var + LN_EPS) * g + b
        Bx, Sx, Dx = x.shape
        N = Bx * Sx
        x_flat = x.reshape(N, Dx)
        x_attn = _layernorm(x_flat, ln_g, ln_b) @ attn_w + attn_b + x_flat
        logits = x_attn @ gate_w
        _ = jax.lax.top_k(logits, TOP_K)
        tpe = N // (MICRO_BATCHES * E)
        g = x_attn.reshape(MICRO_BATCHES, E, tpe, Dx)
        h = jax.nn.gelu(jnp.einsum('metd,edf->metf', g, w1) + b1[None, :, None, :], approximate=False)
        y = jnp.einsum('metf,efd->metd', h, w2) + b2[None, :, None, :]
        out = jax.nn.gelu(y @ next_w + next_b, approximate=False)
        return out.reshape(Bx, Sx, Dx)
    x = x + _L0_xattn_ref(_layernorm(x, axis=-1), ctx_1024, L0_xattn_Wq, L0_xattn_bq, L0_xattn_Wk, L0_xattn_bk, L0_xattn_Wv, L0_xattn_bv)
    x = x + _L0_attn_ref(_layernorm(x, axis=-1), L0_attn_w_qkv, L0_attn_ln_w, L0_attn_w_proj)
    x = x + _L0_ffn_ref(_layernorm(x, axis=-1), L0_ffn_ln_g, L0_ffn_ln_b, L0_ffn_attn_w, L0_ffn_attn_b, L0_ffn_gate_w, L0_ffn_w1, L0_ffn_b1, L0_ffn_w2, L0_ffn_b2, L0_ffn_next_w, L0_ffn_next_b)
    return x

_drawn_inputs = setup_inputs


def setup_inputs(seed=0):
    import zlib

    import numpy as np

    out = dict(_drawn_inputs(seed))
    spreads = {'L0_xattn_bq': (0.0, 0.418),
     'L0_xattn_bk': (0.0, 0.8),
     'L0_xattn_bv': (0.0, 0.1),
     'L0_attn_ln_w': (1.0, 0.2),
     'L0_ffn_ln_g': (1.0, 0.2),
     'L0_ffn_ln_b': (0.0, 0.1),
     'L0_ffn_attn_b': (0.0, 0.1),
     'L0_ffn_b1': (0.0, 0.1),
     'L0_ffn_b2': (0.0, 0.1),
     'L0_ffn_next_b': (0.0, 0.1)}
    factors = {}
    for name, (base, spread) in spreads.items():
        noise = np.random.default_rng([zlib.crc32(name.encode()), seed]).standard_normal(out[name].shape)
        drawn = base * np.exp(spread * noise) if base else spread * noise
        out[name] = jnp.asarray(drawn.astype(out[name].dtype))
    for name, factor in factors.items():
        out[name] = (out[name] * factor).astype(out[name].dtype)
    return out
```

```python
from contextlib import ExitStack

import concourse.bass as bass
from concourse import mybir

F32 = mybir.dt.float32
F32R = mybir.dt.float32r
BF16 = mybir.dt.bfloat16
ACT = mybir.ActivationFunctionType
ALU = mybir.AluOpType
AX = mybir.AxisListType

P = 128
QUAD = 32


def perceiver_block(nc, x, ctx_in, xWq, xbq, xWk, xbk, xWv, xbv, w_qkv, ln_w, w_proj,
                    ln_g, ln_b, attn_w, attn_b, w1, b1, w2, b2, next_w, next_b, out):
    _, TOK, D = x.shape
    J = ctx_in.shape[1]
    E, _, DFF = w1.shape
    TT = TOK // P
    DC = D // P
    CHUNK = 512
    NC = J // CHUNK
    JB = CHUNK // P
    XSCALE = float(D) ** -0.5
    HEADS, LS = 16, 64
    HD = D // HEADS
    ASCALE = float(HD) ** -0.5
    NG = TOK // LS
    HPQ = QUAD // HD
    STRIPS = P // QUAD
    VW = HD + 1
    MICRO = 2
    TPE = TOK // (MICRO * E)
    EG = P // (MICRO * TPE)
    EGN = E // EG
    HALF = 512
    FH = DFF // HALF
    FB = HALF // P
    LN_EPS, RMS_EPS = 1e-5, 1e-6
    MASKED = -1e38
    C_RING, T_RING, PT_RING, PT_BANKS = 3, 2, 3, 4

    with ExitStack() as whole:
        def sem(name):
            return whole.enter_context(nc.semaphore(name))

        def sbuf(name, shape, dt=F32, stack=whole):
            return stack.enter_context(nc.sbuf_tensor(name, shape, dt))

        w1_sb = sbuf("w1_sb", [P, E, DC * DFF])
        raw = sbuf("raw_ctx", [P, NC, JB, D])
        scores = sbuf("scores", [P, NC, TT, CHUNK])
        wv_sb = sbuf("wv_sb", [P, DC, D])
        wqkv_sb = sbuf("wqkv_sb", [P, DC, 3 * D])
        wproj_sb = sbuf("wproj_sb", [P, DC, D])
        attnw_sb = sbuf("attnw_sb", [P, DC, D])
        nextw_sb = sbuf("nextw_sb", [P, DC, D])
        x_sb = sbuf("x_sb", [P, TT, D])
        xres = sbuf("xres", [P, TT, D])
        ident = sbuf("ident", [P, P])
        ident_bf = sbuf("ident_bf", [P, P], BF16)
        causal_bf = sbuf("causal_bf", [P, 8, LS], BF16)
        neg_half = sbuf("neg_half", [P, 4])
        strip_even = sbuf("strip_even", [P, STRIPS])
        parity = sbuf("parity", [P, 2])
        bq_sb = sbuf("bq_sb", [P, DC])
        bk_sb = sbuf("bk_sb", [P, DC])
        lnw_sb = sbuf("lnw_sb", [P, DC])
        lnw_par = sbuf("lnw_par", [P, 2, DC])
        lng_sb = sbuf("lng_sb", [P, DC])
        lnb_sb = sbuf("lnb_sb", [P, DC])
        attnb_sb = sbuf("attnb_sb", [P, DC])
        bn6 = sbuf("bn6", [P, TT, 6])
        mv = sbuf("mv", [P, TT, 2])
        var_eps = sbuf("var_eps", [P, 4])
        rstd = sbuf("rstd", [P, 4])
        qbk = sbuf("qbk", [P, TT])
        chunk_max = sbuf("chunk_max", [P, TT, NC])
        row_max = sbuf("row_max", [P, TT])
        neg_max = sbuf("neg_max", [P, TT])
        chunk_sum = sbuf("chunk_sum", [P, TT, NC])
        row_sum = sbuf("row_sum", [P, TT])
        inv_sum = sbuf("inv_sum", [P, TT])
        head_max = sbuf("head_max", [P, STRIPS, 8])
        inv_den = sbuf("inv_den", [P, 2, TT, 8])
        table_junk = sbuf("table_junk", [P, 1])
        bv_row = sbuf("bv_row", [P, D])

        with ExitStack() as early:
            cH = sbuf("cH", [P, C_RING, JB, D], F32R, early)
            cL = sbuf("cL", [P, C_RING, JB, D], F32R, early)
            tH = sbuf("tH", [P, T_RING, DC, CHUNK], F32R, early)
            tL = sbuf("tL", [P, T_RING, DC, CHUNK], F32R, early)
            pH = sbuf("pH", [P, PT_RING, CHUNK], F32R, early)
            pL = sbuf("pL", [P, PT_RING, CHUNK], F32R, early)
            gH = sbuf("gH", [P, DC, TOK], F32R, early)
            gL = sbuf("gL", [P, DC, TOK], F32R, early)
        with ExitStack() as late:
            b1_sb = sbuf("b1_sb", [P, EGN, DFF], F32, late)
            b2_sb = sbuf("b2_sb", [P, EGN, D], F32, late)
            nextb_sb = sbuf("nextb_sb", [P, D], F32, late)
            wide_a = sbuf("wide_a", [P, 4, 512], F32, late)
            wide_b = sbuf("wide_b", [P, 4, 512], F32, late)
            v2 = sbuf("v2", [P, NG, HEADS, VW], F32, late)
            rows = sbuf("rows", [P, TT, D], F32, late)
            h0 = sbuf("h0", [P, TT, D], F32, late)
            cols = sbuf("cols", [P, DC, TOK], F32, late)
            qn = sbuf("qn", [P, TT, D], F32, late)
            kn = sbuf("kn", [P, TT, D], F32, late)
            qT = sbuf("qT", [P, DC, TOK], F32, late)
            kT = sbuf("kT", [P, 2, DC, TOK], F32, late)
            xaT = sbuf("xaT", [P, DC, TOK], F32, late)
            y_sb = sbuf("y_sb", [P, EGN, D], F32, late)
            yT = sbuf("yT", [P, DC, TOK], F32, late)
            sq_junk = sbuf("sq_junk", [P, D], F32, late)

        pre = scores[:].rearrange("p k t j -> p (k t j)")

        def prelude(n, shape):
            ap = pre[:, n * 512:(n + 1) * 512]
            return ap.rearrange("p (a b) -> p a b", a=shape)
        wq_sb, wk_sb, wkT, xn, xnT, xqT = (prelude(n, 2) for n in range(6))

        scores_w2 = scores[:].rearrange("p (e k) t j -> p e (k t j)", k=2)
        raw_w2 = raw[:].rearrange("p (e k) b d -> p e (k b d)", k=2)

        def w2_of(e):
            ap = scores_w2[:, e] if e < E // 2 else raw_w2[:, e - E // 2]
            return ap.rearrange("p (h b d) -> p h b d", h=FH, b=FB)

        bank = [whole.enter_context(nc.psum_tensor(f"bank{n}", [P, 512], F32)) for n in range(8)]
        t_bank = bank[0:2]
        A_bank = bank[6:8]

        def s_bank(k, t):
            return bank[2 + 2 * (k % 2) + t]

        a_bank = [bank[7], bank[0], bank[1], bank[2]]
        at_bank = bank[3:7]
        y_bank = [bank[7], bank[0]]
        f1_bank = [bank[6], bank[7], bank[0], bank[1]]
        hT_bank = [bank[2], bank[3], bank[6], bank[7]]
        f2_bank = [bank[4], bank[5]]
        yT_bank = [bank[0], bank[1]]
        fin_bank = [bank[2], bank[3]]

        ld_x, ld_wk, ld_wq, ld_bqk, ld_bv, ld_rest, ld_late, stored = (
            sem(n) for n in ("ld_x", "ld_wk", "ld_wq", "ld_bqk", "ld_bv", "ld_rest", "ld_late", "stored"))
        ld_ctx = [sem(f"ld_ctx{k}") for k in range(NC)]
        ld_w1 = [sem(f"ld_w1_{e}") for e in range(E)]
        ld_w2 = [sem(f"ld_w2_{e}") for e in range(E)]
        consts = sem("consts")
        ld_small = sem("ld_small")
        xbv_ready = sem("xbv_ready")
        idbf_ready, lnw_ready = sem("idbf_ready"), sem("lnw_ready")
        var_ready, rstd_ready = sem("var_ready"), sem("rstd_ready")
        norm_ready = sem("norm_ready")
        dve_order = sem("dve_order")
        act_order = sem("act_order")
        wkT_done, wkT_ready = sem("wkT_done"), sem("wkT_ready")
        xnT_done, xnT_ready = sem("xnT_done"), sem("xnT_ready")
        q_done, q_ready = sem("q_done"), sem("q_ready")
        g_done, gH_ready, gL_ready = sem("g_done"), sem("gH_ready"), sem("gL_ready")
        t_done, tH_ready, tL_ready = sem("t_done"), sem("tH_ready"), sem("tL_ready")
        s_done, s_ready = sem("s_done"), sem("s_ready")
        max_ready, p_ready = sem("max_ready"), sem("p_ready")
        cH_ready, cL_ready = sem("cH_ready"), sem("cL_ready")
        pt_done, pH_ready, pL_ready = sem("pt_done"), sem("pH_ready"), sem("pL_ready")
        pv_done = sem("pv_done")
        an_ready, anT_done, anT_ready, xo_done, x1_ready = (
            sem(n) for n in ("an_ready", "anT_done", "anT_ready", "xo_done", "x1_ready"))
        x1T_done, x1T_ready = sem("x1T_done"), sem("x1T_ready")
        qk_done, v_done, v_ready, ones_ready = (sem(n) for n in ("qk_done", "v_done", "v_ready", "ones_ready"))
        sq_ready, qn_ready, kn_ready = sem("sq_ready"), sem("qn_ready"), sem("kn_ready")
        qT_done, kT_done, qT_ready, kT_ready = (sem(n) for n in ("qT_done", "kT_done", "qT_ready", "kT_ready"))
        a_done, a_shifted, a_exp, at_done = (sem(n) for n in ("a_done", "a_shifted", "a_exp", "at_done"))
        at_ready = [sem("at_ready_dve"), sem("at_ready_act")]
        y_done, yn_ready, ynT_done, ynT_ready, proj_done, x2_ready = (
            sem(n) for n in ("y_done", "yn_ready", "ynT_done", "ynT_ready", "proj_done", "x2_ready"))
        h0_ready, h0n_ready, h0T_done, h0T_ready, xa_done, xa_ready = (
            sem(n) for n in ("h0_ready", "h0n_ready", "h0T_done", "h0T_ready", "xa_done", "xa_ready"))
        f1_done, f1_biased, gelu_ready, hT_done, hT_ready, f2_done, f2_ready = (
            sem(n) for n in ("f1_done", "f1_biased", "gelu_ready", "hT_done", "hT_ready", "f2_done", "f2_ready"))
        yT_done, yT_ready, fin_done, fin_biased, fin_gelu, out_ready = (
            sem(n) for n in ("yT_done", "yT_ready", "fin_done", "fin_biased", "fin_gelu", "out_ready"))

        N_REST = 5
        N_SMALL = 4
        N_LATE = E + E + 1

        block = whole.enter_context(nc.Block())

        def halves(w):
            return w.rearrange("(c p) n -> p c n", p=P)

        def per_partition(v):
            return v.rearrange("(c p) -> p c", p=P)

        def row(v):
            return v.rearrange("(a n) -> a n", a=1)

        @block.sync
        def _(sp):
            sp.dma_start(x_sb[:], x[0].rearrange("(t p) d -> p t d", p=P)).then_inc(ld_x, 16)
            sp.dma_start(wk_sb, halves(xWk)).then_inc(ld_wk, 16)
            sp.dma_start(wq_sb, halves(xWq)).then_inc(ld_wq, 16)
            for k in range(NC):
                src = ctx_in[0, k * CHUNK:(k + 1) * CHUNK, :].rearrange("(p b) d -> p (b d)", b=JB)
                sp.dma_start(raw[:, k].rearrange("p b d -> p (b d)"), src).then_inc(ld_ctx[k], 16)
            for dst, src in ((wv_sb, xWv), (wqkv_sb, w_qkv), (wproj_sb, w_proj), (attnw_sb, attn_w),
                             (nextw_sb, next_w)):
                sp.dma_start(dst[:], halves(src)).then_inc(ld_rest, 16)
            for e in range(E):
                sp.dma_start(w1_sb[:, e], w1[e].rearrange("(p c) f -> p (c f)", c=DC)).then_inc(ld_w1[e], 16)
            for half in range(E // 2):
                k = 2 * half + 1
                sp.wait_ge(pt_done, TT * (k + 1))
                sp.dma_start(w2_of(half), w2[half].rearrange("(h p b) d -> p h b d", h=FH, b=FB)).then_inc(ld_w2[half], 16)
                e = half + E // 2
                sp.wait_ge(t_done, DC * NC)
                sp.wait_ge(cH_ready, k + 1)
                sp.wait_ge(cL_ready, k + 1)
                sp.dma_start(w2_of(e), w2[e].rearrange("(h p b) d -> p h b d", h=FH, b=FB)).then_inc(ld_w2[e], 16)
            for t in range(TT):
                sp.wait_ge(out_ready, t + 1)
                sp.dma_start(out[0, t * P:(t + 1) * P, :], xres[:, t, :]).then_inc(stored, 16)
            sp.wait_ge(stored, 16 * TT)

        @block.gpsimd
        def _(pool):
            pool.dma_start(bq_sb[:], per_partition(xbq), allow_slow_non_contiguous=True).then_inc(ld_bqk, 16)
            pool.dma_start(bk_sb[:], per_partition(xbk), allow_slow_non_contiguous=True).then_inc(ld_bqk, 16)
            nc.gpsimd.memset(ident[:], 0.0).then_inc(consts, 1)
            nc.gpsimd.memset(neg_half[:], -0.5).then_inc(consts, 1)
            pool.wait_ge(consts, 2)
            nc.gpsimd.affine_select(out=ident[:], in_=ident[:], compare_op=ALU.not_equal, fill=1.0, base=0,
                                    pattern=[[-1, P]], channel_multiplier=1).then_inc(consts, 1)

            def power(n, width):
                pool.wait_ge(var_ready, n)
                nc.gpsimd.tensor_tensor(rstd[:, 0:width], var_eps[:, 0:width], neg_half[:, 0:width],
                                        ALU.pow).then_inc(rstd_ready, 1)
            power(1, TT)

            nc.gpsimd.memset(causal_bf[:], 0.0).then_inc(consts, 1)
            nc.gpsimd.memset(strip_even[:], 1.0).then_inc(consts, 1)
            for g in range(2):
                pool.wait_ge(consts, 5 + g)
                part = causal_bf[g * LS:(g + 1) * LS]
                nc.gpsimd.affine_select(out=part, in_=part, compare_op=ALU.is_ge, fill=MASKED, base=0,
                                        pattern=[[0, 8], [-1, LS]], channel_multiplier=1).then_inc(consts, 1)
            pool.wait_ge(consts, 7)
            nc.gpsimd.affine_select(out=strip_even[:], in_=strip_even[:], compare_op=ALU.is_ge, fill=0.0, base=0,
                                    pattern=[[-QUAD, STRIPS]], channel_multiplier=1).then_inc(consts, 1)
            pool.wait_ge(consts, 8)
            nc.gpsimd.affine_select(out=strip_even[:], in_=strip_even[:], compare_op=ALU.is_ge, fill=0.0, base=HD - 1,
                                    pattern=[[QUAD, STRIPS]], channel_multiplier=-1).then_inc(consts, 1)
            for dst, v in ((lnw_sb, ln_w),):
                pool.dma_start(dst[:], per_partition(v), allow_slow_non_contiguous=True).then_inc(ld_small, 16)
            for dst, v in ((lng_sb, ln_g), (lnb_sb, ln_b)):
                pool.dma_start(dst[:], per_partition(v), allow_slow_non_contiguous=True).then_inc(ld_small, 16)
            pool.dma_start(attnb_sb[:], attn_b.rearrange("(p c) -> p c", c=DC)).then_inc(ld_small, 16)

            pool.dma_start(bv_row[:], row(xbv).to_broadcast([P, D])).then_inc(ld_bv, 16)
            pool.wait_ge(ld_bv, 16)
            for t in range(TT):
                nc.gpsimd.tensor_tensor(xres[:, t], x_sb[:, t], bv_row[:], ALU.add).then_inc(xbv_ready, 1)

            for k in range(NC):
                pool.wait_ge(cH_ready, k + 1)
                if k >= C_RING:
                    pool.wait_ge(pv_done, TT * (k - C_RING + 1))
                nc.gpsimd.tensor_tensor(cL[:, k % C_RING], raw[:, k], cH[:, k % C_RING].bitcast(F32),
                                        ALU.subtract).then_inc(cL_ready, 1)

            pool.wait_ge(pv_done, TT * NC)
            nc.gpsimd.memset(v2[:], 1.0).then_inc(ones_ready, 1)
            for e in range(E):
                rows_of = slice(QUAD * (e % EG), QUAD * (e % EG + 1))
                pool.dma_start(b1_sb[rows_of, e // EG], b1[e:e + 1, :].to_broadcast([QUAD, DFF])).then_inc(ld_late, 16)
                pool.dma_start(b2_sb[rows_of, e // EG], b2[e:e + 1, :].to_broadcast([QUAD, D])).then_inc(ld_late, 16)
            pool.dma_start(nextb_sb[:], row(next_b).to_broadcast([P, D])).then_inc(ld_late, 16)
            power(2, TT)
            power(3, 4)
            power(4, TT)
            power(5, TT)

        @block.tensor
        def _(pe):
            mm = nc.tensor.matmul

            def transpose(dst, src):
                return nc.tensor.transpose(dst, src, ident[:])

            pe.wait_ge(consts, 3)
            pe.wait_ge(ld_wk, 16)
            for dc in range(DC):
                for c in range(DC):
                    last = transpose(A_bank[0][:, dc * D + c * P:dc * D + (c + 1) * P], wk_sb[:, c, dc * P:(dc + 1) * P])
            last.then_inc(wkT_done, 1)

            def turn_ctx(k):
                pe.wait_ge(ld_ctx[k], 16)
                for c in range(DC):
                    if k >= 1:
                        pe.wait_ge(tL_ready, DC * (k - 1) + c + 1)
                    for b in range(JB):
                        last = transpose(t_bank[c][:, b * P:(b + 1) * P], raw[:, k, b, c * P:(c + 1) * P])
                    last.then_inc(t_done, 1)

            def turn_rows(dst, src, ready, done):
                for t in range(TT):
                    pe.wait_ge(ready, t + 1)
                    for c in range(DC):
                        last = transpose(dst[:, c * TOK + t * P:c * TOK + (t + 1) * P], src[:, t, c * P:(c + 1) * P])
                last.then_inc(done, 1)

            turn_rows(A_bank[1], xn, norm_ready, xnT_done)
            pe.wait_ge(ld_wq, 16)
            pe.wait_ge(xnT_ready, 1)
            for dc in range(DC):
                for c in range(DC):
                    last = mm(bank[2][:, dc * TOK:(dc + 1) * TOK], wq_sb[:, c, dc * P:(dc + 1) * P], xnT[:, c],
                              start=(c == 0), stop=(c == DC - 1))
            last.then_inc(q_done, 1)
            turn_ctx(0)
            pe.wait_ge(wkT_ready, 1)
            pe.wait_ge(q_ready, DC)
            for c in range(DC):
                for dc in range(DC):
                    mm(bank[3][:, c * TOK:(c + 1) * TOK], wkT[:, dc, c * P:(c + 1) * P], xqT[:, dc],
                       start=(dc == 0), stop=(dc == DC - 1))
            for t in range(TT):
                for dc in range(DC):
                    last = mm(bank[4][:, t:t + 1], xqT[:, dc, t * P:(t + 1) * P], bk_sb[:, dc:dc + 1],
                              start=(dc == 0), stop=(dc == DC - 1))
            last.then_inc(g_done, 1)

            for k in range(NC):
                if k + 1 < NC:
                    turn_ctx(k + 1)
                pe.wait_ge(tL_ready, DC * (k + 1))
                if k == 0:
                    pe.wait_ge(gL_ready, 1)
                for t in range(TT):
                    if k >= 2:
                        pe.wait_ge(s_ready, TT * (k - 2) + t + 1)
                    at = slice(t * P, (t + 1) * P)
                    for c in range(DC):
                        mm(s_bank(k, t)[:], gH[:, c, at], tH[:, k % T_RING, c], start=(c == 0), stop=False)
                        mm(s_bank(k, t)[:], gH[:, c, at], tL[:, k % T_RING, c], start=False, stop=False)
                        last = mm(s_bank(k, t)[:], gL[:, c, at], tH[:, k % T_RING, c], start=False, stop=(c == DC - 1))
                    last.then_inc(s_done, 1)

            def turn_p(n):
                k, t = divmod(n, TT)
                pe.wait_ge(p_ready, n + 1)
                if n >= PT_BANKS:
                    pe.wait_ge(pL_ready, n - PT_BANKS + 1)
                for b in range(JB):
                    last = transpose(bank[n % PT_BANKS][:, b * P:(b + 1) * P], scores[:, k, t, b * P:(b + 1) * P])
                last.then_inc(pt_done, 1)

            def weigh(n):
                k, t = divmod(n, TT)
                pe.wait_ge(pL_ready, n + 1)
                pe.wait_ge(cL_ready, k + 1)
                for b in range(JB):
                    for left, right in ((pH, cH), (pH, cL), (pL, cH)):
                        last = mm(A_bank[t][:, 0:D], left[:, n % PT_RING, b * P:(b + 1) * P], right[:, k % C_RING, b],
                                  start=(k == 0 and b == 0 and left is pH and right is cH),
                                  stop=(k == NC - 1 and b == JB - 1 and left is pL))
                last.then_inc(pv_done, 1)

            turn_p(0)
            turn_p(1)
            for n in range(TT * NC):
                if n + 2 < TT * NC:
                    turn_p(n + 2)
                weigh(n)

            turn_rows(bank[4], rows, an_ready, anT_done)
            pe.wait_ge(anT_ready, 1)
            pe.wait_ge(ld_rest, 16 * N_REST)
            for t in range(TT):
                for c in range(DC):
                    last = mm(bank[5][:, t * D:(t + 1) * D], cols[:, c, t * P:(t + 1) * P], wv_sb[:, c],
                              start=(c == 0), stop=(c == DC - 1))
            last.then_inc(xo_done, 1)

            for t in range(TT):
                pe.wait_ge(norm_ready, TT + t + 1)
                for c in range(DC):
                    last = transpose(bank[0][:, c * TOK + t * P:c * TOK + (t + 1) * P], rows[:, t, c * P:(c + 1) * P])
            last.then_inc(x1T_done, 1)
            pe.wait_ge(x1T_ready, 1)
            for t in range(TT):
                for c in range(DC):
                    last = mm(bank[1 + t][:], cols[:, c, t * P:(t + 1) * P], wqkv_sb[:, c, 0:2 * D],
                              start=(c == 0), stop=(c == DC - 1))
                last.then_inc(qk_done, 1)
            for g in range(NG):
                for c in range(DC):
                    for par in range(2):
                        last = mm(bank[3 + g // 2][par * LS:(par + 1) * LS, (g % 2) * D:(g % 2 + 1) * D],
                                  cols[:, c, g * LS:(g + 1) * LS], wqkv_sb[:, c, 2 * D:3 * D],
                                  start=(c == 0), stop=(c == DC - 1))
                if g % 2:
                    last.then_inc(v_done, 1)
            turn_rows(bank[5], qn, qn_ready, qT_done)
            turn_rows(bank[6], kn, kn_ready, kT_done)

            pe.wait_ge(idbf_ready, 1)
            for i in range(STRIPS):
                mm(a_bank[i][:], ident_bf[:], causal_bf[:].rearrange("p a k -> p (a k)"), start=True, stop=False,
                   skip_group_check=True)
            pe.wait_ge(qT_ready, DC)
            pe.wait_ge(kT_ready, 2 * DC)
            for t in range(TT):
                for c in range(DC):
                    for par in range(2):
                        for g in range(2):
                            for i in range(STRIPS):
                                strip = slice(i * QUAD, (i + 1) * QUAD)
                                tok = slice(t * P + g * LS, t * P + (g + 1) * LS)
                                at = ((t * DC + c) * 2 + par) * LS
                                last = mm(a_bank[i][g * LS:(g + 1) * LS, at:at + LS], qT[strip, c, tok],
                                          kT[strip, par, c, tok], start=False, stop=True, skip_group_check=True)
            last.then_inc(a_done, 1)
            for i in range(STRIPS):
                pe.wait_ge(a_exp, i + 1)
                if i == 0:
                    pe.wait_ge(v_ready, 2)
                if i == 2:
                    pe.wait_ge(qT_ready, DC)
                for tc in range(4):
                    last = transpose(at_bank[i][:, tc * P:(tc + 1) * P], wide_a[:, i, tc * P:(tc + 1) * P])
                last.then_inc(at_done, 1)
            pe.wait_ge(a_shifted, 2)
            for i in range(STRIPS):
                pe.wait_ge(at_ready[i % 2], i // 2 + 1)
                for t in range(TT):
                    for c in range(DC):
                        for g in range(2):
                            for par in range(2):
                                half = slice(par * LS, (par + 1) * LS)
                                q_at = (t * DC + c) * P + g * LS
                                at = (t * 8 + c * STRIPS + i) * VW
                                last = mm(y_bank[par][g * LS:(g + 1) * LS, at:at + VW],
                                          wide_b[half, i, q_at:q_at + LS], v2[half, t * 2 + g, 8 * c + 2 * i + par],
                                          start=True, stop=True)
            last.then_inc(y_done, 1)
            pe.wait_ge(yn_ready, 2)
            turn_rows(bank[1], rows, yn_ready, ynT_done)
            pe.wait_ge(ynT_ready, 1)
            for t in range(TT):
                for c in range(DC):
                    last = mm(bank[2][:, t * D:(t + 1) * D], cols[:, c, t * P:(t + 1) * P], wproj_sb[:, c],
                              start=(c == 0), stop=(c == DC - 1))
            last.then_inc(proj_done, 1)

            pe.wait_ge(h0_ready, TT)
            for dc in range(DC):
                for t in range(TT):
                    mm(bank[4 + dc][:, t * P:(t + 1) * P], h0[:, t, dc:D:DC], ident[:], start=(t == 0), stop=False,
                       skip_group_check=True)
            turn_rows(bank[3], rows, h0n_ready, h0T_done)
            pe.wait_ge(h0T_ready, DC)
            for dc in range(DC):
                for c in range(DC):
                    last = mm(bank[4 + dc][:, 0:TOK], attnw_sb[:, c, dc:D:DC], cols[:, c], start=False,
                              stop=(c == DC - 1), skip_group_check=True)
                last.then_inc(xa_done, 1)

            def first(g, h):
                n = g * FH + h
                if n == 0:
                    pe.wait_ge(xa_ready, DC)
                for dc in range(DC):
                    for j in range(EG):
                        e = g * EG + j
                        if h == 0 and dc == 0:
                            pe.wait_ge(ld_w1[e], 16)
                        last = mm(f1_bank[n][j * QUAD:(j + 1) * QUAD, :], xaT[:, dc, e * QUAD:(e + 1) * QUAD],
                                  w1_sb[:, e, dc * DFF + h * HALF:dc * DFF + (h + 1) * HALF],
                                  start=(dc == 0), stop=(dc == DC - 1))
                last.then_inc(f1_done, 1)

            def turn_h(g, h):
                n = g * FH + h
                pe.wait_ge(gelu_ready, n + 1)
                for b in range(FB):
                    last = transpose(hT_bank[n][:, b * P:(b + 1) * P], wide_a[:, n, b:HALF:FB])
                last.then_inc(hT_done, 1)

            def second(g, h):
                n = g * FH + h
                pe.wait_ge(hT_ready, n + 1)
                for b in range(FB):
                    for j in range(EG):
                        e = g * EG + j
                        if b == 0 and h == 0:
                            pe.wait_ge(ld_w2[e], 16)
                        last = mm(f2_bank[g][j * QUAD:(j + 1) * QUAD, 0:D],
                                  wide_b[:, n, b * P + j * QUAD:b * P + (j + 1) * QUAD], w2_of(e)[:, h, b],
                                  start=(h == 0 and b == 0), stop=(h == FH - 1 and b == FB - 1))
                if h == FH - 1:
                    last.then_inc(f2_done, 1)

            def turn_y(g):
                pe.wait_ge(f2_ready, g + 1)
                for c in range(DC):
                    last = transpose(yT_bank[g][:, c * P:(c + 1) * P], y_sb[:, g, c * P:(c + 1) * P])
                last.then_inc(yT_done, 1)

            first(0, 0)
            first(0, 1)
            turn_h(0, 0)
            first(1, 0)
            turn_h(0, 1)
            first(1, 1)
            second(0, 0)
            turn_h(1, 0)
            second(0, 1)
            turn_h(1, 1)
            second(1, 0)
            turn_y(0)
            second(1, 1)
            turn_y(1)
            pe.wait_ge(yT_ready, EGN)
            for t in range(TT):
                for c in range(DC):
                    last = mm(fin_bank[t][:, 0:D], yT[:, c, t * P:(t + 1) * P], nextw_sb[:, c],
                              start=(c == 0), stop=(c == DC - 1))
                last.then_inc(fin_done, 1)

        @block.scalar
        def _(act):
            A = nc.scalar.activation
            act.wait_ge(consts, 2)
            A(rstd[:, 3:4], neg_half[:, 3:4], ACT.Exp).then_inc(act_order, 1)
            act.wait_ge(wkT_done, 1)
            A(wkT, A_bank[0][:].rearrange("p (a b) -> p a b", a=2), ACT.Copy).then_inc(wkT_ready, 1)

            def high_ctx(k):
                for c in range(DC):
                    act.wait_ge(t_done, DC * k + c + 1)
                    if k >= T_RING and c == 0:
                        act.wait_ge(s_done, TT * (k - T_RING + 1))
                    A(tH[:, k % T_RING, c], t_bank[c][:], ACT.Copy).then_inc(tH_ready, 1)
            high_ctx(0)
            act.wait_ge(g_done, 1)
            A(gH[:].rearrange("p c i -> p (c i)"), bank[3][:], ACT.Copy).then_inc(gH_ready, 1)
            for k in range(1, NC):
                high_ctx(k)

            def exps(n):
                k, t = divmod(n, TT)
                act.wait_ge(max_ready, 1)
                A(scores[:, k, t], scores[:, k, t], ACT.Exp, bias=neg_max[:, t:t + 1], scale=XSCALE,
                  accum_out=chunk_sum[:, t, k:k + 1]).then_inc(p_ready, 1)
            exps(0)
            exps(1)
            for n in range(TT * NC):
                if n + 2 < TT * NC:
                    exps(n + 2)
                act.wait_ge(pt_done, n + 1)
                if n >= PT_RING:
                    act.wait_ge(pv_done, n - PT_RING + 1)
                A(pH[:, n % PT_RING], bank[n % PT_BANKS][:], ACT.Copy).then_inc(pH_ready, 1)

            act.wait_ge(anT_done, 1)
            A(cols[:].rearrange("p c i -> p (c i)"), bank[4][:], ACT.Copy).then_inc(anT_ready, 1)
            act.wait_ge(x1T_done, 1)
            A(cols[:].rearrange("p c i -> p (c i)"), bank[0][:], ACT.Copy).then_inc(x1T_ready, 1)
            for t in range(TT):
                act.wait_ge(qk_done, t + 1)
                for s in range(2):
                    if t + s:
                        act.wait_ge(sq_ready, 2 * t + s)
                    A(sq_junk[:], bank[1 + t][:, s * D:(s + 1) * D], ACT.Square, scale=float(D) ** -0.5,
                      accum_out=var_eps[:, 2 * t + s:2 * t + s + 1]).then_inc(sq_ready, 1)
            act.wait_ge(ones_ready, 1)
            for h in range(2):
                if h == 0:
                    act.wait_ge(v_done, 1)
                else:
                    act.wait_ge(v_done, 2)
                A(v2[:, 2 * h:2 * h + 2, :, 0:HD], bank[3 + h][:].rearrange("p (g n e) -> p g n e", g=2, e=HD),
                  ACT.Copy).then_inc(v_ready, 1)
            act.wait_ge(kT_done, 1)
            act.wait_ge(lnw_ready, 1)
            for c in range(DC):
                A(kT[:, 0, c], bank[6][:, c * TOK:(c + 1) * TOK], ACT.Copy, scale=lnw_par[:, 0, c:c + 1]).then_inc(kT_ready, 1)
            for i in range(STRIPS):
                act.wait_ge(a_shifted, i + 1)
                A(wide_a[:, i], wide_a[:, i], ACT.Exp, scale=ASCALE).then_inc(a_exp, 1)
            for i in (1, 3):
                act.wait_ge(at_done, i + 1)
                A(wide_b[:, i], at_bank[i][:], ACT.Copy).then_inc(at_ready[1], 1)
            A(table_junk[:], neg_half[:, 0:1], ACT.Gelu).then_inc(act_order, 1)
            act.wait_ge(ynT_done, 1)
            A(cols[:].rearrange("p c i -> p (c i)"), bank[1][:], ACT.Copy).then_inc(ynT_ready, 1)
            for n in range(EGN * FH):
                act.wait_ge(f1_biased, n + 1)
                A(wide_a[:, n], wide_a[:, n], ACT.Gelu).then_inc(gelu_ready, 1)
            for t in range(TT):
                act.wait_ge(fin_biased, t + 1)
                A(rows[:, t], rows[:, t], ACT.Gelu).then_inc(fin_gelu, 1)

        @block.vector
        def _(dve):
            V = nc.vector
            steps = [0]

            def chain(ins):
                steps[0] += 1
                ins.then_inc(dve_order, 1)
                dve.wait_ge(dve_order, steps[0])

            def moments(src, first_read=None):
                for t in range(TT):
                    if first_read:
                        first_read(t)
                    chain(V.bn_stats(bn6[:, t], src[:, t]))
                    chain(V.bn_aggr(mv[:, t], bn6[:, t]))

            norms = [0, 0]

            def layernorm(dst, src, done, eps=LN_EPS, first_read=None):
                moments(src, first_read)
                V.tensor_scalar(var_eps[:, 0:TT], mv[:, :, 1], eps, None, ALU.add).then_inc(var_ready, 1)
                norms[0] += 1
                dve.wait_ge(rstd_ready, norms[0])
                for t in range(TT):
                    V.tensor_scalar(dst[:, t], src[:, t], mv[:, t, 0:1], rstd[:, t:t + 1], ALU.subtract,
                                    ALU.mult).then_inc(done, 1)

            dve.wait_ge(ld_x, 16)
            layernorm(xn, x_sb, norm_ready)
            dve.wait_ge(xnT_done, 1)
            V.tensor_copy(xnT, A_bank[1][:].rearrange("p (a b) -> p a b", a=2)).then_inc(xnT_ready, 1)
            dve.wait_ge(ld_bqk, 32)
            dve.wait_ge(q_done, 1)
            for c in range(DC):
                V.tensor_scalar(xqT[:, c], bank[2][:, c * TOK:(c + 1) * TOK], bq_sb[:, c:c + 1], None,
                                ALU.add).then_inc(q_ready, 1)

            def low_ctx(k):
                for c in range(DC):
                    dve.wait_ge(tH_ready, DC * k + c + 1)
                    V.tensor_tensor(tL[:, k % T_RING, c], t_bank[c][:], tH[:, k % T_RING, c].bitcast(F32),
                                    ALU.subtract).then_inc(tL_ready, 1)

            def high_rows(k):
                dve.wait_ge(ld_ctx[k], 16)
                if k >= C_RING:
                    dve.wait_ge(pv_done, TT * (k - C_RING + 1))
                V.tensor_copy(cH[:, k % C_RING], raw[:, k]).then_inc(cH_ready, 1)

            low_ctx(0)
            dve.wait_ge(gH_ready, 1)
            V.tensor_tensor(gL[:], bank[3][:].rearrange("p (c i) -> p c i", c=DC), gH[:].bitcast(F32),
                            ALU.subtract).then_inc(gL_ready, 1)
            chain(V.tensor_copy(qbk[:], bank[4][:, 0:TT]))
            for k in range(NC):
                if k + 1 < NC:
                    low_ctx(k + 1)
                if 1 <= k <= C_RING:
                    high_rows(k - 1)
                for t in range(TT):
                    dve.wait_ge(s_done, TT * k + t + 1)
                    V.tensor_scalar(scores[:, k, t], s_bank(k, t)[:], qbk[:, t:t + 1], None, ALU.add, ALU.max,
                                    accum_out=chunk_max[:, t, k:k + 1]).then_inc(s_ready, 1)
            dve.wait_ge(s_ready, TT * NC)
            chain(V.tensor_reduce(row_max[:], chunk_max[:], AX.X, ALU.max))
            V.tensor_scalar(neg_max[:], row_max[:], -XSCALE, None, ALU.mult).then_inc(max_ready, 1)
            for n in range(TT * NC):
                k, t = divmod(n, TT)
                dve.wait_ge(pH_ready, n + 1)
                V.tensor_tensor(pL[:, n % PT_RING], bank[n % PT_BANKS][:], pH[:, n % PT_RING].bitcast(F32),
                                ALU.subtract).then_inc(pL_ready, 1)
                if n >= 3 and (n - 3) % TT == 0:
                    kk = C_RING + (n - 3) // TT
                    if kk < NC:
                        high_rows(kk)
            dve.wait_ge(p_ready, TT * NC)
            chain(V.tensor_reduce(row_sum[:], chunk_sum[:], AX.X, ALU.add))
            chain(V.reciprocal(inv_sum[:], row_sum[:]))
            dve.wait_ge(pv_done, TT * NC)
            for t in range(TT):
                V.tensor_scalar(rows[:, t], A_bank[t][:, 0:D], inv_sum[:, t:t + 1], None, ALU.mult).then_inc(an_ready, 1)
            dve.wait_ge(consts, 9)
            dve.wait_ge(ld_small, 16 * N_SMALL)
            chain(V.tensor_reduce(parity[:, 0:1], strip_even[:], AX.X, ALU.add))
            chain(V.tensor_scalar(parity[:, 1:2], parity[:, 0:1], -1.0, 1.0, ALU.mult, ALU.add))
            V.tensor_scalar(lnw_par[:, 0], lnw_sb[:], parity[:, 0:1], None, ALU.mult).then_inc(lnw_ready, 1)
            chain(V.tensor_scalar(lnw_par[:, 1], lnw_sb[:], parity[:, 1:2], None, ALU.mult))
            V.tensor_copy(ident_bf[:], ident[:]).then_inc(idbf_ready, 1)
            dve.wait_ge(xo_done, 1)
            dve.wait_ge(xbv_ready, TT)
            for t in range(TT):
                chain(V.tensor_tensor(x_sb[:, t], bank[5][:, t * D:(t + 1) * D], xres[:, t], ALU.add))
            layernorm(rows, x_sb, norm_ready)
            dve.wait_ge(sq_ready, 4)
            V.tensor_scalar(var_eps[:], var_eps[:], RMS_EPS, None, ALU.add).then_inc(var_ready, 1)
            norms[0] += 1
            dve.wait_ge(rstd_ready, norms[0])
            for t in range(TT):
                V.tensor_scalar(qn[:, t], bank[1 + t][:, 0:D], rstd[:, 2 * t:2 * t + 1], None, ALU.mult).then_inc(qn_ready, 1)
            for t in range(TT):
                V.tensor_scalar(kn[:, t], bank[1 + t][:, D:2 * D], rstd[:, 2 * t + 1:2 * t + 2], None,
                                ALU.mult).then_inc(kn_ready, 1)
            dve.wait_ge(qT_done, 1)
            for c in range(DC):
                V.tensor_scalar(qT[:, c], bank[5][:, c * TOK:(c + 1) * TOK], lnw_sb[:, c:c + 1], None,
                                ALU.mult).then_inc(qT_ready, 1)
            dve.wait_ge(kT_ready, DC)
            for c in range(DC):
                V.tensor_scalar(kT[:, 1, c], bank[6][:, c * TOK:(c + 1) * TOK], lnw_par[:, 1, c:c + 1], None,
                                ALU.mult).then_inc(kT_ready, 1)
            dve.wait_ge(a_done, 1)
            for i in range(STRIPS):
                heads = a_bank[i][:].rearrange("p (a k) -> p a k", k=LS)
                chain(V.tensor_reduce(head_max[:, i], heads, AX.X, ALU.max))
                V.tensor_tensor(wide_a[:, i].rearrange("p (a k) -> p a k", k=LS), heads,
                                head_max[:, i].unsqueeze(2).to_broadcast([P, 8, LS]), ALU.subtract).then_inc(a_shifted, 1)
            for i in (0, 2):
                dve.wait_ge(at_done, i + 1)
                V.tensor_copy(wide_b[:, i], at_bank[i][:]).then_inc(at_ready[0], 1)
            dve.wait_ge(y_done, 1)
            for par in range(2):
                y = y_bank[par][:, 0:TT * 8 * VW].rearrange("p (t n e) -> p t n e", t=TT, e=VW)
                chain(V.reciprocal(inv_den[:, par], y[:, :, :, HD]))
                dst = rows[:].rearrange("p t (n r e) -> p t n r e", r=2, e=HD)[:, :, :, par]
                V.tensor_tensor(dst, y[:, :, :, 0:HD], inv_den[:, par].unsqueeze(3).to_broadcast([P, TT, 8, HD]),
                                ALU.mult).then_inc(yn_ready, 1)
            dve.wait_ge(proj_done, 1)
            for t in range(TT):
                chain(V.tensor_tensor(xres[:, t], bank[2][:, t * D:(t + 1) * D], x_sb[:, t], ALU.add))
            layernorm(h0, xres, h0_ready)
            dve.wait_ge(h0_ready, TT)
            layernorm(rows, h0, h0n_ready)
            dve.wait_ge(h0T_done, 1)
            for c in range(DC):
                V.tensor_scalar(cols[:, c], bank[3][:, c * TOK:(c + 1) * TOK], lng_sb[:, c:c + 1], lnb_sb[:, c:c + 1],
                                ALU.mult, ALU.add).then_inc(h0T_ready, 1)
            for c in range(DC):
                dve.wait_ge(xa_done, c + 1)
                V.tensor_scalar(xaT[:, c].rearrange("p (e m t) -> p m e t", m=MICRO, t=TPE),
                                bank[4 + c][:, 0:TOK].rearrange("p (m e t) -> p m e t", m=MICRO, t=TPE),
                                attnb_sb[:, c:c + 1], None, ALU.add).then_inc(xa_ready, 1)
            dve.wait_ge(ld_late, 16 * N_LATE)

            def bias1(n):
                dve.wait_ge(f1_done, n + 1)
                V.tensor_tensor(wide_a[:, n], f1_bank[n][:],
                                b1_sb[:, n // FH, (n % FH) * HALF:(n % FH + 1) * HALF], ALU.add).then_inc(f1_biased, 1)

            def keep_h(n):
                dve.wait_ge(hT_done, n + 1)
                V.tensor_copy(wide_b[:, n], hT_bank[n][:]).then_inc(hT_ready, 1)

            def bias2(g):
                dve.wait_ge(f2_done, g + 1)
                V.tensor_tensor(y_sb[:, g], f2_bank[g][:, 0:D], b2_sb[:, g], ALU.add).then_inc(f2_ready, 1)

            def keep_y(g):
                dve.wait_ge(yT_done, g + 1)
                dst = yT[:].rearrange("p c (m e t) -> p c m e t", m=MICRO, t=TPE)
                for c in range(DC):
                    ins = V.tensor_copy(dst[:, c, :, g * EG:(g + 1) * EG],
                                        yT_bank[g][:, c * P:(c + 1) * P].rearrange("p (e m t) -> p m e t", m=MICRO, t=TPE))
                    if c == DC - 1:
                        ins.then_inc(yT_ready, 1)

            bias1(0)
            bias1(1)
            keep_h(0)
            bias1(2)
            keep_h(1)
            bias1(3)
            keep_h(2)
            keep_h(3)
            bias2(0)
            keep_y(0)
            bias2(1)
            keep_y(1)
            for t in range(TT):
                dve.wait_ge(fin_done, t + 1)
                V.tensor_tensor(rows[:, t], fin_bank[t][:, 0:D], nextb_sb[:], ALU.add).then_inc(fin_biased, 1)
            for t in range(TT):
                dve.wait_ge(fin_gelu, t + 1)
                V.tensor_tensor(xres[:, t], xres[:, t], rows[:, t], ALU.add).then_inc(out_ready, 1)


_INS = ["x", "ctx_1024", "L0_xattn_Wq", "L0_xattn_bq", "L0_xattn_Wk", "L0_xattn_bk", "L0_xattn_Wv", "L0_xattn_bv",
        "L0_attn_w_qkv", "L0_attn_ln_w", "L0_attn_w_proj", "L0_ffn_ln_g", "L0_ffn_ln_b", "L0_ffn_attn_w",
        "L0_ffn_attn_b", "L0_ffn_w1", "L0_ffn_b1", "L0_ffn_w2", "L0_ffn_b2", "L0_ffn_next_w", "L0_ffn_next_b"]


def kernel(**inputs):
    import numpy as _np
    import concourse.bacc as _bacc
    from concourse import mybir as _mybir
    from concourse.bass_utils import run_bass_kernel_spmd as _run

    nc = _bacc.Bacc("TRN2", target_bir_lowering=False, num_devices=1)
    arrays, args = {}, []
    for name in _INS:
        a = _np.ascontiguousarray(inputs[name])
        arrays[f"in_{name}"] = a
        args.append(nc.dram_tensor(f"in_{name}", a.shape, _mybir.dt.from_np(a.dtype), kind="ExternalInput").ap())
    args.append(nc.dram_tensor("out_x", (1, 256, 256), _mybir.dt.float32, kind="ExternalOutput").ap())
    perceiver_block(nc, *args)
    r = _run(nc, [arrays], core_ids=[0])
    return r.results[0]["out_x"]
```

```python
from contextlib import ExitStack

import concourse.bass as bass
from concourse import mybir

F32 = mybir.dt.float32
F32R = mybir.dt.float32r
BF16 = mybir.dt.bfloat16
ACT = mybir.ActivationFunctionType
ALU = mybir.AluOpType
AX = mybir.AxisListType

P = 128
QUAD = 32


def perceiver_block(nc, x, ctx_in, xWq, xbq, xWk, xbk, xWv, xbv, w_qkv, ln_w, w_proj,
                    ln_g, ln_b, attn_w, attn_b, w1, b1, w2, b2, next_w, next_b, out):
    _, TOK, D = x.shape
    J = ctx_in.shape[1]
    E, _, DFF = w1.shape
    TT = TOK // P
    DC = D // P
    CHUNK = 512
    NC = J // CHUNK
    JB = CHUNK // P
    XSCALE = float(D) ** -0.5
    HEADS, LS = 16, 64
    HD = D // HEADS
    ASCALE = float(HD) ** -0.5
    GT = P // LS
    STRIPS = P // QUAD
    PAIRS = HEADS // 2
    VW = HD + 1
    MICRO = TT
    TPE = TOK // (MICRO * E)
    EG = P // (MICRO * TPE)
    EGN = E // EG
    HALF = 512
    FH = DFF // HALF
    FB = HALF // P
    LN_EPS, RMS_EPS = 1e-5, 1e-6
    MASKED = -1e38
    RAW_RING, T_RING, P_RING, PT_BANKS = 3, 2, 3, 2
    W1_EARLY = 5
    SLOT = DC * DFF

    with ExitStack() as whole:
        def sem(name):
            return whole.enter_context(nc.semaphore(name))

        def sbuf(name, shape, dt=F32, stack=whole):
            return stack.enter_context(nc.sbuf_tensor(name, shape, dt))

        w1_early = sbuf("w1_early", [P, W1_EARLY, SLOT])
        wv_sb = sbuf("wv_sb", [P, DC, D])
        wqkv_sb = sbuf("wqkv_sb", [P, DC, 3 * D])
        wproj_sb = sbuf("wproj_sb", [P, DC, D])
        attnw_sb = sbuf("attnw_sb", [P, DC, D])
        nextw_sb = sbuf("nextw_sb", [P, DC, D])
        x_sb = sbuf("x_sb", [P, TT, D])
        xres = sbuf("xres", [P, TT, D])
        xaT = sbuf("xaT", [P, DC, TOK])
        bv_row = sbuf("bv_row", [P, D])
        ident = sbuf("ident", [P, P])
        ident_bf = sbuf("ident_bf", [P, P], BF16)
        causal_bf = sbuf("causal_bf", [P, 4, LS], BF16)
        warm_bf = sbuf("warm_bf", [P, 512], BF16)
        neg_half = sbuf("neg_half", [P, 2])
        strip_even = sbuf("strip_even", [P, STRIPS])
        parity = sbuf("parity", [P, 2])
        bq_sb = sbuf("bq_sb", [P, DC])
        bk_sb = sbuf("bk_sb", [P, DC])
        lnw_sb = sbuf("lnw_sb", [P, DC])
        lnw_par = sbuf("lnw_par", [P, DC, 2])
        lng_sb = sbuf("lng_sb", [P, DC])
        lnb_sb = sbuf("lnb_sb", [P, DC])
        attnb_sb = sbuf("attnb_sb", [P, DC])
        bn6 = sbuf("bn6", [P, TT, 6])
        mv = sbuf("mv", [P, TT, 2])
        var_eps = sbuf("var_eps", [P, TT, 2])
        mean_sq = sbuf("mean_sq", [P, TT, 2])
        rstd = sbuf("rstd", [P, TT, 2])
        qbk = sbuf("qbk", [P, TT])
        chunk_max = sbuf("chunk_max", [P, TT, NC])
        row_max = sbuf("row_max", [P, TT])
        neg_max = sbuf("neg_max", [P, TT])
        chunk_sum = sbuf("chunk_sum", [P, TT, NC])
        row_sum = sbuf("row_sum", [P, TT])
        inv_sum = sbuf("inv_sum", [P, TT])
        head_max = sbuf("head_max", [P, TT, STRIPS, 4])
        inv_den = sbuf("inv_den", [P, TT, HEADS])
        table_junk = sbuf("table_junk", [P, 1])

        with ExitStack() as early:
            cH = sbuf("cH", [P, NC, JB, D], F32R, early)
            cL = sbuf("cL", [P, NC, JB, D], F32R, early)
            scores1 = sbuf("scores1", [P, NC, CHUNK], F32, early)
            pH = sbuf("pH", [P, P_RING, CHUNK], F32R, early)
            pL = sbuf("pL", [P, P_RING, CHUNK], F32R, early)
            scores0 = sbuf("scores0", [P, NC, CHUNK], F32, early)
            tH = sbuf("tH", [P, T_RING, DC, CHUNK], F32R, early)
            tL = sbuf("tL", [P, T_RING, DC, CHUNK], F32R, early)
            raw = sbuf("raw_ctx", [P, RAW_RING, JB, D], F32, early)
            gH = sbuf("gH", [P, DC, TOK], F32R, early)
            gL = sbuf("gL", [P, DC, TOK], F32R, early)
        with ExitStack() as late:
            over_cH = sbuf("over_cH", [P, 4, SLOT], F32, late)
            over_cL = sbuf("over_cL", [P, 4, SLOT], F32, late)
            over_scores1 = sbuf("over_scores1", [P, 2, SLOT], F32, late)
            over_p = sbuf("over_p", [P, 2 * P_RING * CHUNK], F32, late)
            b1_sb = sbuf("b1_sb", [P, EGN, DFF], F32, late)
            b2_sb = sbuf("b2_sb", [P, EGN, D], F32, late)
            nextb_sb = sbuf("nextb_sb", [P, D], F32, late)
            h0 = sbuf("h0", [P, TT, D], F32, late)
            sbuf("rest_of_scores0", [P, NC * CHUNK - EGN * DFF - EGN * D - D - TT * D], F32, late)
            wide_a = sbuf("wide_a", [P, 4, 512], F32, late)
            wide_b = sbuf("wide_b", [P, 4, 512], F32, late)
            v2 = sbuf("v2", [P, TT, GT, PAIRS, 2, VW], F32, late)
            rows = sbuf("rows", [P, TT, D], F32, late)
            cols = sbuf("cols", [P, TT, DC, P], F32, late)
            qT = sbuf("qT", [P, TT, DC, P], F32, late)
            kT = sbuf("kT", [P, TT, DC, 2, P], F32, late)

        scores = [scores0, scores1]
        pre = scores1[:].rearrange("p k j -> p (k j)")

        def prelude(n):
            return pre[:, (n + 2) * 512:(n + 3) * 512].rearrange("p (a b) -> p a b", a=2)
        wq_sb, wk_sb, wkT, xn, xnT, xqT = (prelude(n) for n in range(6))

        spare = wide_b[:].rearrange("p a b -> p (a b)").rearrange("p (t s d) -> p t s d", t=TT, s=4)

        places = [(over_cH[:, 0], 2), (over_cL[:, 0], 2), (over_cH[:, 1], 4), (over_cL[:, 1], 4),
                  (over_scores1[:, 0], 4), (over_cH[:, 2], 6), (over_cL[:, 2], 6), (over_cH[:, 3], 8),
                  (over_cL[:, 3], 8), (over_scores1[:, 1], 8), (over_p[:, 0:SLOT], 8)]
        W1_LATE = E - W1_EARLY

        def w1_of(e):
            return w1_early[:, e] if e < W1_EARLY else places[e - W1_EARLY][0]

        def w2_of(e):
            return places[W1_LATE + e][0].rearrange("p (h b d) -> p h b d", h=FH, b=FB)

        psum = whole.enter_context(nc.psum_tensor("psum", [P, 8, 512], F32))
        bank = [psum[:, n] for n in range(8)]
        A_bank = bank[6:8]

        def s_bank(k, t):
            return bank[2 + 2 * (k % 2) + t]

        an_bank, xo_bank, x1_bank = [bank[2], bank[0]], [bank[3], bank[1]], [bank[4], bank[0]]
        qk_bank, v_bank, qkT_bank = [bank[5], bank[1]], [bank[6], bank[2]], [bank[2], bank[7]]
        a_first = [3, 0]
        at_bank = [[bank[2], bank[3]], [bank[7], bank[0]]]
        y_bank, yn_bank, proj_bank = [bank[4], bank[1]], [bank[5], bank[2]], [bank[6], bank[3]]
        h0_bank, xa_bank = [bank[5], bank[2]], [bank[6], bank[3]]
        f1_bank = [bank[4], bank[7], bank[0], bank[1]]
        hT_bank = [bank[2], bank[5], bank[4], bank[7]]
        f2_bank, yT_bank, fin_bank = [bank[6], bank[3]], [bank[0], bank[1]], [bank[2], bank[5]]

        ld_x, ld_wk, ld_wq, ld_bqk, ld_bv, ld_small, ld_rest, ld_late, stored = (
            sem(n) for n in ("ld_x", "ld_wk", "ld_wq", "ld_bqk", "ld_bv", "ld_small", "ld_rest", "ld_late", "stored"))
        ld_ctx = [sem(f"ld_ctx{k}") for k in range(NC)]
        ld_w1 = [sem(f"ld_w1_{e}") for e in range(E)]
        ld_w2 = [sem(f"ld_w2_{e}") for e in range(E)]
        consts = sem("consts")
        warm_ready, xbv_ready, idbf_ready, lnw_ready = (
            sem(n) for n in ("warm_ready", "xbv_ready", "idbf_ready", "lnw_ready"))
        var_ready = [sem(f"var_ready{t}") for t in range(TT)]
        rstd_ready = [sem(f"rstd_ready{t}") for t in range(TT)]
        xn_ready, x1n_ready, dve_order, act_order = (
            sem(n) for n in ("xn_ready", "x1n_ready", "dve_order", "act_order"))
        wkT_done, wkT_ready, xnT_done, xnT_ready = (
            sem(n) for n in ("wkT_done", "wkT_ready", "xnT_done", "xnT_ready"))
        q_done, q_ready, g_done, qbk_done = (sem(n) for n in ("q_done", "q_ready", "g_done", "qbk_done"))
        gH_ready, gL_ready = sem("gH_ready"), sem("gL_ready")
        t_done, tH_ready, tL_ready = sem("t_done"), sem("tH_ready"), sem("tL_ready")
        s_done, s_ready, max_ready = sem("s_done"), sem("s_ready"), sem("max_ready")
        cH_ready, cL_ready = sem("cH_ready"), sem("cL_ready")
        p_ready, pt_done, pH_ready, pL_ready, pv_done = (
            sem(n) for n in ("p_ready", "pt_done", "pH_ready", "pL_ready", "pv_done"))
        an_ready, anT_done, anT_ready, xo_done, x1T_done, x1T_ready = (
            sem(n) for n in ("an_ready", "anT_done", "anT_ready", "xo_done", "x1T_done", "x1T_ready"))
        qk_done, v_done, v_ready, ones_ready = (sem(n) for n in ("qk_done", "v_done", "v_ready", "ones_ready"))
        sq_ready, qkn_ready, qkT_done, qT_ready, kT_ready = (
            sem(n) for n in ("sq_ready", "qkn_ready", "qkT_done", "qT_ready", "kT_ready"))
        a_done, a_max, a_shifted, a_exp, at_done, at_ready = (
            sem(n) for n in ("a_done", "a_max", "a_shifted", "a_exp", "at_done", "at_ready"))
        y_done, yn_ready, ynT_done, ynT_ready, proj_done = (
            sem(n) for n in ("y_done", "yn_ready", "ynT_done", "ynT_ready", "proj_done"))
        h0_ready, h0n_ready, h0T_done, h0T_ready, xa_done, xa_ready = (
            sem(n) for n in ("h0_ready", "h0n_ready", "h0T_done", "h0T_ready", "xa_done", "xa_ready"))
        f1_done, f1_biased, gelu_ready, hT_done, hT_ready, f2_done, f2_ready = (
            sem(n) for n in ("f1_done", "f1_biased", "gelu_ready", "hT_done", "hT_ready", "f2_done", "f2_ready"))
        yT_done, yT_ready, fin_done, fin_biased, fin_gelu, out_ready = (
            sem(n) for n in ("yT_done", "yT_ready", "fin_done", "fin_biased", "fin_gelu", "out_ready"))

        N_REST, N_SMALL, N_LATE = 5, 4, 2 * E + 1

        block = whole.enter_context(nc.Block())

        def halves(w):
            return w.rearrange("(c p) n -> p c n", p=P)

        def per_partition(v):
            return v.rearrange("(c p) -> p c", p=P)

        def row(v):
            return v.rearrange("(a n) -> a n", a=1)

        @block.sync
        def _(sp):
            def load_ctx(k):
                if k >= RAW_RING:
                    sp.wait_ge(t_done, DC * (k - RAW_RING + 1))
                    sp.wait_ge(cH_ready, k - RAW_RING + 1)
                    sp.wait_ge(cL_ready, k - RAW_RING + 1)
                src = ctx_in[0, k * CHUNK:(k + 1) * CHUNK, :].rearrange("(p b) d -> p (b d)", b=JB)
                sp.dma_start(raw[:, k % RAW_RING].rearrange("p b d -> p (b d)"), src).then_inc(ld_ctx[k], 16)

            def load_w1(e):
                sp.dma_start(w1_of(e), w1[e].rearrange("(p c) f -> p (c f)", c=DC)).then_inc(ld_w1[e], 16)

            sp.dma_start(x_sb[:], x[0].rearrange("(t p) d -> p t d", p=P)).then_inc(ld_x, 16)
            sp.dma_start(wk_sb, halves(xWk)).then_inc(ld_wk, 16)
            for k in range(RAW_RING):
                load_ctx(k)
            for dst, src in ((wv_sb, xWv), (wqkv_sb, w_qkv), (wproj_sb, w_proj), (attnw_sb, attn_w),
                             (nextw_sb, next_w)):
                sp.dma_start(dst[:], halves(src)).then_inc(ld_rest, 16)
            for k in range(RAW_RING, NC):
                load_ctx(k)
                if k < NC - 2:
                    load_w1(k - RAW_RING)
            for e in range(NC - 2 - RAW_RING, W1_EARLY):
                load_w1(e)
            sp.wait_ge(pt_done, NC)
            for g in range(EGN):
                for j in range(EG):
                    e = g * EG + j
                    strip = slice(j * QUAD, (j + 1) * QUAD)
                    sp.dma_start(b1_sb[strip, g], b1[e:e + 1, :].to_broadcast([QUAD, DFF])).then_inc(ld_late, 16)
                    sp.dma_start(b2_sb[strip, g], b2[e:e + 1, :].to_broadcast([QUAD, D])).then_inc(ld_late, 16)
            sp.dma_start(nextb_sb[:], row(next_b).to_broadcast([P, D])).then_inc(ld_late, 16)
            for n, (_, used) in enumerate(places):
                sp.wait_ge(pv_done, NC + used)
                if n < W1_LATE:
                    load_w1(W1_EARLY + n)
                else:
                    e = n - W1_LATE
                    sp.dma_start(w2_of(e), w2[e].rearrange("(h p b) d -> p h b d", h=FH, b=FB)).then_inc(ld_w2[e], 16)
            for t in range(TT):
                sp.wait_ge(out_ready, t + 1)
                sp.dma_start(out[0, t * P:(t + 1) * P, :], xres[:, t, :]).then_inc(stored, 16)
            sp.wait_ge(stored, 16 * TT)

        @block.gpsimd
        def _(pool):
            nc.gpsimd.memset(ident[:], 0.0).then_inc(consts, 1)
            nc.gpsimd.memset(neg_half[:], -0.5).then_inc(consts, 1)
            pool.dma_start(bq_sb[:], per_partition(xbq), allow_slow_non_contiguous=True).then_inc(ld_bqk, 16)
            pool.dma_start(bk_sb[:], per_partition(xbk), allow_slow_non_contiguous=True).then_inc(ld_bqk, 16)
            pool.wait_ge(consts, 2)
            nc.gpsimd.affine_select(out=ident[:], in_=ident[:], compare_op=ALU.not_equal, fill=1.0, base=0,
                                    pattern=[[-1, P]], channel_multiplier=1).then_inc(consts, 1)

            powers = [0, 0]

            def power(t, width):
                powers[t] += 1
                pool.wait_ge(var_ready[t], powers[t])
                nc.gpsimd.tensor_tensor(rstd[:, t, 0:width], var_eps[:, t, 0:width], neg_half[:, 0:width],
                                        ALU.pow).then_inc(rstd_ready[t], 1)
            power(0, 1)
            power(1, 1)
            pool.dma_start(bv_row[:], row(xbv).to_broadcast([P, D])).then_inc(ld_bv, 16)
            pool.dma_start(lnw_sb[:], per_partition(ln_w), allow_slow_non_contiguous=True).then_inc(ld_small, 16)
            pool.dma_start(lng_sb[:], per_partition(ln_g), allow_slow_non_contiguous=True).then_inc(ld_small, 16)
            pool.dma_start(lnb_sb[:], per_partition(ln_b), allow_slow_non_contiguous=True).then_inc(ld_small, 16)
            pool.dma_start(attnb_sb[:], attn_b.rearrange("(p c) -> p c", c=DC)).then_inc(ld_small, 16)

            def low_rows(k):
                pool.wait_ge(cH_ready, k + 1)
                nc.gpsimd.tensor_tensor(cL[:, k], raw[:, k % RAW_RING], cH[:, k].bitcast(F32),
                                        ALU.subtract).then_inc(cL_ready, 1)

            low_rows(0)
            low_rows(1)
            nc.gpsimd.memset(causal_bf[:], 0.0).then_inc(consts, 1)
            nc.gpsimd.memset(strip_even[:], 1.0).then_inc(consts, 1)
            for g in range(2):
                pool.wait_ge(consts, 5 + g)
                part = causal_bf[g * LS:(g + 1) * LS]
                nc.gpsimd.affine_select(out=part, in_=part, compare_op=ALU.is_ge, fill=MASKED, base=0,
                                        pattern=[[0, 4], [-1, LS]], channel_multiplier=1).then_inc(consts, 1)
            pool.wait_ge(consts, 7)
            nc.gpsimd.affine_select(out=strip_even[:], in_=strip_even[:], compare_op=ALU.is_ge, fill=0.0, base=0,
                                    pattern=[[-QUAD, STRIPS]], channel_multiplier=1).then_inc(consts, 1)
            pool.wait_ge(consts, 8)
            nc.gpsimd.affine_select(out=strip_even[:], in_=strip_even[:], compare_op=ALU.is_ge, fill=0.0, base=HD - 1,
                                    pattern=[[QUAD, STRIPS]], channel_multiplier=-1).then_inc(consts, 1)
            for k in range(2, NC):
                low_rows(k)
            pool.wait_ge(ld_bv, 16)
            for t in range(TT):
                nc.gpsimd.tensor_tensor(xres[:, t], x_sb[:, t], bv_row[:], ALU.add).then_inc(xbv_ready, 1)
            pool.wait_ge(s_done, TT * NC)
            pool.wait_ge(cL_ready, NC)
            nc.gpsimd.memset(v2[:], 0.0).then_inc(ones_ready, 1)
            pool.wait_ge(ones_ready, 1)
            for par in range(2):
                nc.gpsimd.memset(v2[par * LS:(par + 1) * LS, :, :, :, par, HD], 1.0).then_inc(ones_ready, 1)
                pool.wait_ge(ones_ready, 2 + par)
            power(0, 1)
            power(0, 2)
            power(1, 1)
            power(0, 1)
            power(1, 2)
            power(0, 1)
            power(1, 1)
            power(1, 1)

        @block.tensor
        def _(pe):
            mm = nc.tensor.matmul

            def transpose(dst, src):
                return nc.tensor.transpose(dst, src, ident[:])

            def warm(dst, n):
                for _ in range(n):
                    mm(dst, warm_bf[:, 0:P], warm_bf[:], start=True, stop=True)

            pe.wait_ge(warm_ready, 1)
            warm(bank[5], 7)
            pe.wait_ge(consts, 3)
            pe.wait_ge(ld_wk, 16)
            for dc in range(DC):
                for c in range(DC):
                    last = transpose(A_bank[0][:, dc * D + c * P:dc * D + (c + 1) * P], wk_sb[:, c, dc * P:(dc + 1) * P])
            last.then_inc(wkT_done, 1)
            warm(bank[5], 2)

            def turn_ctx(k):
                pe.wait_ge(ld_ctx[k], 16)
                for c in range(DC):
                    if k >= 1:
                        pe.wait_ge(tL_ready, DC * (k - 1) + c + 1)
                    for b in range(JB):
                        last = transpose(bank[c][:, b * P:(b + 1) * P], raw[:, k % RAW_RING, b, c * P:(c + 1) * P])
                    last.then_inc(t_done, 1)

            for t in range(TT):
                pe.wait_ge(xn_ready, t + 1)
                for c in range(DC):
                    last = transpose(A_bank[1][:, c * TOK + t * P:c * TOK + (t + 1) * P], xn[:, t, c * P:(c + 1) * P])
            last.then_inc(xnT_done, 1)
            turn_ctx(0)
            pe.wait_ge(ld_wq, 16)
            pe.wait_ge(xnT_ready, 1)
            for dc in range(DC):
                for c in range(DC):
                    last = mm(bank[2 + dc][:, 0:TOK], wq_sb[:, c, dc * P:(dc + 1) * P], xnT[:, c],
                              start=(c == 0), stop=(c == DC - 1))
                last.then_inc(q_done, 1)
            pe.wait_ge(wkT_ready, 1)
            for dc in range(DC):
                pe.wait_ge(q_ready, dc + 1)
                for c in range(DC):
                    last = mm(bank[4 + c][:, 0:TOK], wkT[:, dc, c * P:(c + 1) * P], xqT[:, dc],
                              start=(dc == 0), stop=(dc == DC - 1))
            last.then_inc(g_done, 1)
            for t in range(TT):
                for dc in range(DC):
                    last = mm(A_bank[1][:, t:t + 1], xqT[:, dc, t * P:(t + 1) * P], bk_sb[:, dc:dc + 1],
                              start=(dc == 0), stop=(dc == DC - 1))
            last.then_inc(qbk_done, 1)

            for k in range(NC):
                if k + 1 < NC:
                    turn_ctx(k + 1)
                pe.wait_ge(tL_ready, DC * (k + 1))
                if k == 0:
                    pe.wait_ge(gL_ready, 1)
                for t in range(TT):
                    if k >= 2:
                        pe.wait_ge(s_ready, TT * (k - 2) + t + 1)
                    at = slice(t * P, (t + 1) * P)
                    for c in range(DC):
                        mm(s_bank(k, t), gH[:, c, at], tH[:, k % T_RING, c], start=(c == 0), stop=False)
                        mm(s_bank(k, t), gH[:, c, at], tL[:, k % T_RING, c], start=False, stop=False)
                        last = mm(s_bank(k, t), gL[:, c, at], tH[:, k % T_RING, c], start=False, stop=(c == DC - 1))
                    last.then_inc(s_done, 1)

            def turn_p(n):
                t, k = divmod(n, NC)
                pe.wait_ge(p_ready, n + 1)
                if n >= PT_BANKS:
                    pe.wait_ge(pL_ready, n - PT_BANKS + 1)
                for b in range(JB):
                    last = transpose(bank[n % PT_BANKS][:, b * P:(b + 1) * P], scores[t][:, k, b * P:(b + 1) * P])
                last.then_inc(pt_done, 1)

            def weigh(n, half):
                t, k = divmod(n, NC)
                if half == 0:
                    pe.wait_ge(pL_ready, n + 1)
                    pe.wait_ge(cL_ready, k + 1)
                for b in range(half * JB // 2, (half + 1) * JB // 2):
                    for left, right in ((pH, cH), (pH, cL), (pL, cH)):
                        last = mm(A_bank[t][:, 0:D], left[:, n % P_RING, b * P:(b + 1) * P], right[:, k, b],
                                  start=(k == 0 and b == 0 and left is pH and right is cH),
                                  stop=(k == NC - 1 and b == JB - 1 and left is pL))
                if half:
                    last.then_inc(pv_done, 1)

            def turn_rows(t, dst, src, ready, done):
                pe.wait_ge(ready, t + 1)
                for c in range(DC):
                    last = transpose(dst[:, c * P:(c + 1) * P], src[:, c * P:(c + 1) * P])
                last.then_inc(done, 1)

            def turn_an(t):
                turn_rows(t, an_bank[t], rows[:, t], an_ready, anT_done)

            def xattn_out(t):
                pe.wait_ge(anT_ready, t + 1)
                if t == 0:
                    pe.wait_ge(ld_rest, 16 * N_REST)
                for c in range(DC):
                    last = mm(xo_bank[t][:, 0:D], cols[:, t, c], wv_sb[:, c], start=(c == 0), stop=(c == DC - 1))
                last.then_inc(xo_done, 1)

            def turn_x1(t):
                turn_rows(t, x1_bank[t], rows[:, t], x1n_ready, x1T_done)

            def project_qk(t):
                pe.wait_ge(x1T_ready, t + 1)
                for c in range(DC):
                    last = mm(qk_bank[t], cols[:, t, c], wqkv_sb[:, c, 0:2 * D], start=(c == 0), stop=(c == DC - 1))
                last.then_inc(qk_done, 1)

            def project_v(t):
                for g in range(GT):
                    for c in range(DC):
                        for par in range(2):
                            last = mm(v_bank[t][par * LS:(par + 1) * LS, g * D:(g + 1) * D],
                                      cols[:, t, c, g * LS:(g + 1) * LS], wqkv_sb[:, c, 2 * D:3 * D],
                                      start=(c == 0), stop=(c == DC - 1))
                last.then_inc(v_done, 1)

            def turn_qk(t):
                pe.wait_ge(qkn_ready, t + 1)
                for s in range(2):
                    for c in range(DC):
                        at = (s * DC + c) * P
                        last = transpose(qkT_bank[t][:, at:at + P], spare[:, t, s, c * P:(c + 1) * P])
                last.then_inc(qkT_done, 1)

            def self_scores(t):
                pe.wait_ge(idbf_ready, 1)
                pe.wait_ge(qkn_ready, t + 1)
                pe.wait_ge(v_ready, 2 * (t + 1))
                for i in range(STRIPS):
                    mm(bank[a_first[t] + i][:, 0:4 * LS], ident_bf[:], causal_bf[:].rearrange("p a k -> p (a k)"),
                       start=True, stop=False, skip_group_check=True)
                pe.wait_ge(qT_ready, DC * (t + 1))
                pe.wait_ge(kT_ready, t + 1)
                for c in range(DC):
                    for i in range(STRIPS):
                        strip = slice(i * QUAD, (i + 1) * QUAD)
                        for g in range(GT):
                            tok = slice(g * LS, (g + 1) * LS)
                            last = mm(bank[a_first[t] + i][tok, c * 2 * LS:(c + 1) * 2 * LS], qT[strip, t, c, tok],
                                      kT[strip, t, c, :, tok], start=False, stop=True, skip_group_check=True)
                last.then_inc(a_done, 1)

            def turn_a(t, h):
                pe.wait_ge(a_exp, 2 * t + h + 1)
                for i in range(2):
                    for c in range(DC):
                        at = (i * DC + c) * P
                        last = transpose(at_bank[t][h][:, at:at + P], wide_a[:, 2 * t + h, at:at + P])
                last.then_inc(at_done, 1)

            def self_values(t, h):
                pe.wait_ge(at_ready, 2 * t + h + 1)
                for i in range(2):
                    for c in range(DC):
                        pair = c * STRIPS + 2 * h + i
                        for g in range(GT):
                            at = (i * DC + c) * P + g * LS
                            last = mm(y_bank[t][g * LS:(g + 1) * LS, pair * 2 * VW:(pair + 1) * 2 * VW],
                                      wide_b[:, 2 * t + h, at:at + LS],
                                      v2[:, t, g, pair].rearrange("p r e -> p (r e)"), start=True, stop=True)
                if h:
                    last.then_inc(y_done, 1)

            def turn_yn(t):
                turn_rows(t, yn_bank[t], rows[:, t], yn_ready, ynT_done)

            def project_y(t):
                pe.wait_ge(ynT_ready, t + 1)
                for c in range(DC):
                    last = mm(proj_bank[t][:, 0:D], cols[:, t, c], wproj_sb[:, c], start=(c == 0), stop=(c == DC - 1))
                last.then_inc(proj_done, 1)

            def add_h0(t):
                pe.wait_ge(h0_ready, t + 1)
                for dc in range(DC):
                    mm(xa_bank[t][:, dc * P:(dc + 1) * P], h0[:, t, dc:D:DC], ident[:], start=(dc == 0), stop=False,
                       skip_group_check=True)

            def turn_h0n(t):
                turn_rows(t, h0_bank[t], rows[:, t], h0n_ready, h0T_done)

            def x_attn(t):
                pe.wait_ge(h0T_ready, t + 1)
                for dc in range(DC):
                    for c in range(DC):
                        last = mm(xa_bank[t][:, dc * P:(dc + 1) * P], attnw_sb[:, c, dc:D:DC], cols[:, t, c],
                                  start=False, stop=(c == DC - 1), skip_group_check=True)
                last.then_inc(xa_done, 1)

            turn_p(0)
            turn_p(1)
            for k in range(NC):
                weigh(k, 0)
                turn_p(k + 2)
                weigh(k, 1)
            for k in range(NC):
                n = NC + k
                weigh(n, 0)
                if n + 2 < TT * NC:
                    turn_p(n + 2)
                if k == 1:
                    xattn_out(0)
                if k == 3:
                    project_qk(0)
                if k == 5:
                    turn_qk(0)
                if k == 7:
                    turn_a(0, 0)
                weigh(n, 1)
                if k == 0:
                    turn_an(0)
                if k == 2:
                    turn_x1(0)
                if k == 3:
                    project_v(0)
                if k == 6:
                    self_scores(0)
            turn_a(0, 1)
            self_values(0, 0)
            turn_an(1)
            self_values(0, 1)
            xattn_out(1)
            turn_yn(0)
            warm(bank[7], 2)
            project_y(0)
            turn_x1(1)
            warm(bank[7], 2)
            project_qk(1)
            project_v(1)
            add_h0(0)
            turn_qk(1)
            turn_h0n(0)
            self_scores(1)
            x_attn(0)
            warm(bank[4], 6)
            turn_a(1, 0)
            turn_a(1, 1)
            self_values(1, 0)
            self_values(1, 1)
            turn_yn(1)
            warm(bank[4], 2)
            project_y(1)
            warm(bank[4], 6)
            add_h0(1)
            warm(bank[4], 6)
            turn_h0n(1)
            warm(bank[4], 2)
            x_attn(1)

            def first(g, h):
                n = g * FH + h
                if n == 0:
                    pe.wait_ge(xa_ready, TT)
                for dc in range(DC):
                    for j in range(EG):
                        e = g * EG + j
                        if h == 0 and dc == 0:
                            pe.wait_ge(ld_w1[e], 16)
                        last = mm(f1_bank[n][j * QUAD:(j + 1) * QUAD, :], xaT[:, dc, e * QUAD:(e + 1) * QUAD],
                                  w1_of(e)[:, dc * DFF + h * HALF:dc * DFF + (h + 1) * HALF],
                                  start=(dc == 0), stop=(dc == DC - 1))
                last.then_inc(f1_done, 1)

            def turn_h(g, h):
                n = g * FH + h
                pe.wait_ge(gelu_ready, n + 1)
                for b in range(FB):
                    last = transpose(hT_bank[n][:, b * P:(b + 1) * P], wide_a[:, n, b:HALF:FB])
                last.then_inc(hT_done, 1)

            def second(g, h):
                n = g * FH + h
                pe.wait_ge(hT_ready, n + 1)
                for b in range(FB):
                    for j in range(EG):
                        e = g * EG + j
                        if b == 0 and h == 0:
                            pe.wait_ge(ld_w2[e], 16)
                        last = mm(f2_bank[g][j * QUAD:(j + 1) * QUAD, 0:D],
                                  wide_b[:, n, b * P + j * QUAD:b * P + (j + 1) * QUAD], w2_of(e)[:, h, b],
                                  start=(h == 0 and b == 0), stop=(h == FH - 1 and b == FB - 1))
                if h == FH - 1:
                    last.then_inc(f2_done, 1)

            def turn_y(g):
                pe.wait_ge(f2_ready, g + 1)
                for c in range(DC):
                    last = transpose(yT_bank[g][:, c * P:(c + 1) * P], h0[:, g, c * P:(c + 1) * P])
                last.then_inc(yT_done, 1)

            first(0, 0)
            first(0, 1)
            turn_h(0, 0)
            first(1, 0)
            turn_h(0, 1)
            first(1, 1)
            second(0, 0)
            turn_h(1, 0)
            second(0, 1)
            turn_h(1, 1)
            second(1, 0)
            turn_y(0)
            second(1, 1)
            turn_y(1)
            pe.wait_ge(yT_ready, 2 * EGN)
            for t in range(TT):
                for c in range(DC):
                    last = mm(fin_bank[t][:, 0:D], qT[:, t, c], nextw_sb[:, c], start=(c == 0), stop=(c == DC - 1))
                last.then_inc(fin_done, 1)

        @block.scalar
        def _(act):
            A = nc.scalar.activation
            act.dma_start(wq_sb, halves(xWq)).then_inc(ld_wq, 16)
            act.wait_ge(warm_ready, 1)
            A(table_junk[:], warm_bf[:, 0:1], ACT.Exp).then_inc(act_order, 1)
            act.wait_ge(wkT_done, 1)
            A(wkT, A_bank[0].rearrange("p (a b) -> p a b", a=2), ACT.Copy).then_inc(wkT_ready, 1)

            def high_ctx(k):
                for c in range(DC):
                    act.wait_ge(t_done, DC * k + c + 1)
                    if k >= T_RING and c == 0:
                        act.wait_ge(s_done, TT * (k - T_RING + 1))
                    A(tH[:, k % T_RING, c], bank[c], ACT.Copy).then_inc(tH_ready, 1)

            def high_rows(k):
                act.wait_ge(ld_ctx[k], 16)
                A(cH[:, k], raw[:, k % RAW_RING], ACT.Copy).then_inc(cH_ready, 1)

            high_ctx(0)
            high_rows(0)
            act.wait_ge(g_done, 1)
            A(gH[:], psum[:, 4:6, 0:TOK], ACT.Copy).then_inc(gH_ready, 1)
            for k in range(1, NC):
                high_ctx(k)
                high_rows(k)

            def exps(n):
                t, k = divmod(n, NC)
                if n == 0:
                    act.wait_ge(max_ready, 1)
                A(scores[t][:, k], scores[t][:, k], ACT.Exp, bias=neg_max[:, t:t + 1], scale=XSCALE,
                  accum_out=chunk_sum[:, t, k:k + 1]).then_inc(p_ready, 1)

            def high_p(n):
                act.wait_ge(pt_done, n + 1)
                if n >= P_RING:
                    act.wait_ge(pv_done, n - P_RING + 1)
                A(pH[:, n % P_RING], bank[n % PT_BANKS], ACT.Copy).then_inc(pH_ready, 1)

            def keep_cols(t, src, done, ready):
                act.wait_ge(done, t + 1)
                A(cols[:, t], src[:, 0:D].rearrange("p (c i) -> p c i", c=DC), ACT.Copy).then_inc(ready, 1)

            def keep_an(t):
                keep_cols(t, an_bank[t], anT_done, anT_ready)

            def keep_x1(t):
                keep_cols(t, x1_bank[t], x1T_done, x1T_ready)

            def squares(t):
                act.wait_ge(qk_done, t + 1)
                for s in range(2):
                    if s:
                        act.wait_ge(sq_ready, 2 * t + 1)
                    A(spare[:, t, 2], qk_bank[t][:, s * D:(s + 1) * D], ACT.Square, scale=float(D) ** -0.5,
                      accum_out=mean_sq[:, t, s:s + 1]).then_inc(sq_ready, 1)

            def keep_v(t):
                act.wait_ge(v_done, t + 1)
                act.wait_ge(ones_ready, 3)
                for par in range(2):
                    half = slice(par * LS, (par + 1) * LS)
                    src = v_bank[t][half, :].rearrange("p (g n r e) -> p g n r e", g=GT, r=2, e=HD)[:, :, :, par]
                    A(v2[half, t, :, :, par, 0:HD], src, ACT.Copy).then_inc(v_ready, 1)

            def keep_q(t):
                act.wait_ge(qkT_done, t + 1)
                act.wait_ge(lnw_ready, 1)
                for c in range(DC):
                    A(qT[:, t, c], qkT_bank[t][:, c * P:(c + 1) * P], ACT.Copy,
                      scale=lnw_sb[:, c:c + 1]).then_inc(qT_ready, 1)

            def self_exp(t, h):
                act.wait_ge(a_shifted, 2 * t + h + 1)
                A(wide_a[:, 2 * t + h], wide_a[:, 2 * t + h], ACT.Exp, scale=ASCALE).then_inc(a_exp, 1)

            def keep_a(t, h):
                act.wait_ge(at_done, 2 * t + h + 1)
                A(wide_b[:, 2 * t + h], at_bank[t][h], ACT.Copy).then_inc(at_ready, 1)

            def keep_yn(t):
                keep_cols(t, yn_bank[t], ynT_done, ynT_ready)

            for n in range(3):
                exps(n)
            for n in range(NC):
                high_p(n)
                exps(n + 3)
            for k in range(NC):
                high_p(NC + k)
                if k + 3 < NC:
                    exps(NC + k + 3)
                if k == 0:
                    keep_an(0)
                if k == 3:
                    keep_x1(0)
                if k == 4:
                    squares(0)
                if k == 5:
                    keep_v(0)
                if k == 6:
                    keep_q(0)
            self_exp(0, 0)
            self_exp(0, 1)
            keep_a(0, 0)
            keep_a(0, 1)
            keep_an(1)
            keep_yn(0)
            keep_x1(1)
            squares(1)
            keep_v(1)
            keep_q(1)
            self_exp(1, 0)
            self_exp(1, 1)
            A(table_junk[:], warm_bf[:, 0:1], ACT.Gelu).then_inc(act_order, 1)
            keep_a(1, 0)
            keep_a(1, 1)
            keep_yn(1)
            for n in range(EGN * FH):
                act.wait_ge(f1_biased, n + 1)
                A(wide_a[:, n], wide_a[:, n], ACT.Gelu).then_inc(gelu_ready, 1)
            for t in range(TT):
                act.wait_ge(fin_biased, t + 1)
                A(rows[:, t], rows[:, t], ACT.Gelu).then_inc(fin_gelu, 1)

        @block.vector
        def _(dve):
            V = nc.vector
            steps = [0]
            norms = [0] * TT

            def counted(ins):
                steps[0] += 1
                ins.then_inc(dve_order, 1)
                return steps[0]

            def chain(ins):
                dve.wait_ge(dve_order, counted(ins))

            def variance(t, src):
                chain(V.bn_stats(bn6[:, t], src))
                chain(V.bn_aggr(mv[:, t], bn6[:, t]))
                V.tensor_scalar(var_eps[:, t, 0:1], mv[:, t, 1:2], LN_EPS, None, ALU.add).then_inc(var_ready[t], 1)

            def normed(t, dst, src, done):
                norms[t] += 1
                dve.wait_ge(rstd_ready[t], norms[t])
                V.tensor_scalar(dst, src, mv[:, t, 0:1], rstd[:, t, 0:1], ALU.subtract, ALU.mult).then_inc(done, 1)

            V.memset(warm_bf[:], 0.0).then_inc(warm_ready, 1)
            dve.wait_ge(ld_x, 16)
            first_stats = [counted(V.bn_stats(bn6[:, t], x_sb[:, t])) for t in range(TT)]
            for t in range(TT):
                dve.wait_ge(dve_order, first_stats[t])
                first_stats[t] = counted(V.bn_aggr(mv[:, t], bn6[:, t]))
            for t in range(TT):
                dve.wait_ge(dve_order, first_stats[t])
                V.tensor_scalar(var_eps[:, t, 0:1], mv[:, t, 1:2], LN_EPS, None, ALU.add).then_inc(var_ready[t], 1)
            for t in range(TT):
                normed(t, xn[:, t], x_sb[:, t], xn_ready)
            dve.wait_ge(xnT_done, 1)
            V.tensor_copy(xnT, A_bank[1].rearrange("p (a b) -> p a b", a=2)).then_inc(xnT_ready, 1)

            def low_ctx(k):
                for c in range(DC):
                    dve.wait_ge(tH_ready, DC * k + c + 1)
                    V.tensor_tensor(tL[:, k % T_RING, c], bank[c], tH[:, k % T_RING, c].bitcast(F32),
                                    ALU.subtract).then_inc(tL_ready, 1)

            low_ctx(0)
            dve.wait_ge(ld_bqk, 32)
            for c in range(DC):
                dve.wait_ge(q_done, c + 1)
                V.tensor_scalar(xqT[:, c], bank[2 + c][:, 0:TOK], bq_sb[:, c:c + 1], None, ALU.add).then_inc(q_ready, 1)
            dve.wait_ge(gH_ready, 1)
            V.tensor_tensor(gL[:], psum[:, 4:6, 0:TOK], gH[:].bitcast(F32), ALU.subtract).then_inc(gL_ready, 1)
            dve.wait_ge(qbk_done, 1)
            chain(V.tensor_copy(qbk[:], A_bank[1][:, 0:TT]))
            for k in range(NC):
                if k + 1 < NC:
                    low_ctx(k + 1)
                for t in range(TT):
                    dve.wait_ge(s_done, TT * k + t + 1)
                    V.tensor_scalar(scores[t][:, k], s_bank(k, t), qbk[:, t:t + 1], None, ALU.add, ALU.max,
                                    accum_out=chunk_max[:, t, k:k + 1]).then_inc(s_ready, 1)
            dve.wait_ge(s_ready, TT * NC)
            chain(V.tensor_reduce(row_max[:], chunk_max[:], AX.X, ALU.max))
            V.tensor_scalar(neg_max[:], row_max[:], -XSCALE, None, ALU.mult).then_inc(max_ready, 1)

            dve.wait_ge(consts, 9)
            dve.wait_ge(ld_small, 16 * N_SMALL)
            chain(V.tensor_reduce(parity[:, 0:1], strip_even[:], AX.X, ALU.add))
            chain(V.tensor_scalar(parity[:, 1:2], parity[:, 0:1], -1.0, 1.0, ALU.mult, ALU.add))
            for par in range(2):
                V.tensor_scalar(lnw_par[:, :, par], lnw_sb[:], parity[:, par:par + 1], None, ALU.mult).then_inc(lnw_ready, 1)
            V.tensor_copy(ident_bf[:], ident[:]).then_inc(idbf_ready, 1)

            def low_p(n):
                dve.wait_ge(pH_ready, n + 1)
                V.tensor_tensor(pL[:, n % P_RING], bank[n % PT_BANKS], pH[:, n % P_RING].bitcast(F32),
                                ALU.subtract).then_inc(pL_ready, 1)

            def sum_rows(t):
                dve.wait_ge(p_ready, NC * (t + 1))
                chain(V.tensor_reduce(row_sum[:, t:t + 1], chunk_sum[:, t], AX.X, ALU.add))
                chain(V.reciprocal(inv_sum[:, t:t + 1], row_sum[:, t:t + 1]))

            def divide_an(t):
                dve.wait_ge(pv_done, NC * (t + 1))
                V.tensor_scalar(rows[:, t], A_bank[t][:, 0:D], inv_sum[:, t:t + 1], None, ALU.mult).then_inc(an_ready, 1)

            def add_xattn(t):
                dve.wait_ge(xo_done, t + 1)
                dve.wait_ge(xbv_ready, TT)
                chain(V.tensor_tensor(x_sb[:, t], xo_bank[t][:, 0:D], xres[:, t], ALU.add))
                variance(t, x_sb[:, t])

            def norm_x1(t):
                normed(t, rows[:, t], x_sb[:, t], x1n_ready)

            def mean_squares(t):
                dve.wait_ge(sq_ready, 2 * (t + 1))
                V.tensor_scalar(var_eps[:, t], mean_sq[:, t], RMS_EPS, None, ALU.add).then_inc(var_ready[t], 1)

            def norm_qk(t):
                norms[t] += 1
                dve.wait_ge(rstd_ready[t], norms[t])
                V.tensor_tensor(spare[:, t, 0:2], qk_bank[t].rearrange("p (s d) -> p s d", s=2),
                                rstd[:, t].unsqueeze(2).to_broadcast([P, 2, D]), ALU.mult).then_inc(qkn_ready, 1)

            def keep_k(t):
                dve.wait_ge(qT_ready, DC * (t + 1))
                dve.wait_ge(lnw_ready, 2)
                src = qkT_bank[t][:, DC * P:2 * DC * P].rearrange("p (c i) -> p c i", c=DC)
                for c in range(DC):
                    ins = V.tensor_tensor(kT[:, t, c], src[:, c].unsqueeze(1).to_broadcast([P, 2, P]),
                                          lnw_par[:, c].unsqueeze(2).to_broadcast([P, 2, P]), ALU.mult)
                ins.then_inc(kT_ready, 1)

            def shift_scores(t):
                dve.wait_ge(a_done, t + 1)

                def strips(h):
                    first = a_first[t] + 2 * h
                    return psum[:, first:first + 2, 0:4 * LS].rearrange("p i (a k) -> p i a k", k=LS)

                def top(h):
                    V.tensor_reduce(head_max[:, t, 2 * h:2 * h + 2], strips(h), AX.X, ALU.max).then_inc(a_max, 1)

                def shift(h):
                    dve.wait_ge(a_max, 2 * t + h + 1)
                    dst = wide_a[:, 2 * t + h].rearrange("p (i a k) -> p i a k", i=2, k=LS)
                    for i in range(2):
                        ins = V.tensor_tensor(dst[:, i], strips(h)[:, i],
                                              head_max[:, t, 2 * h + i].unsqueeze(2).to_broadcast([P, 4, LS]),
                                              ALU.subtract)
                    ins.then_inc(a_shifted, 1)
                return top, shift

            def divide_y(t):
                dve.wait_ge(y_done, t + 1)
                y = y_bank[t][:, 0:HEADS * VW].rearrange("p (n e) -> p n e", e=VW)
                chain(V.reciprocal(inv_den[:, t], y[:, :, HD]))
                V.tensor_tensor(rows[:, t].rearrange("p (n e) -> p n e", e=HD), y[:, :, 0:HD],
                                inv_den[:, t].unsqueeze(2).to_broadcast([P, HEADS, HD]), ALU.mult).then_inc(yn_ready, 1)

            def add_self(t):
                dve.wait_ge(proj_done, t + 1)
                chain(V.tensor_tensor(xres[:, t], proj_bank[t][:, 0:D], x_sb[:, t], ALU.add))
                variance(t, xres[:, t])

            def norm_x2(t):
                normed(t, h0[:, t], xres[:, t], h0_ready)
                dve.wait_ge(h0_ready, t + 1)
                variance(t, h0[:, t])

            def norm_h0(t):
                normed(t, rows[:, t], h0[:, t], h0n_ready)

            def keep_h0(t):
                dve.wait_ge(h0T_done, t + 1)
                for c in range(DC):
                    ins = V.tensor_scalar(cols[:, t, c], h0_bank[t][:, c * P:(c + 1) * P], lng_sb[:, c:c + 1],
                                          lnb_sb[:, c:c + 1], ALU.mult, ALU.add)
                ins.then_inc(h0T_ready, 1)

            def keep_xa(t):
                dve.wait_ge(xa_done, t + 1)
                V.tensor_tensor(xaT[:].rearrange("p c (e m i) -> p c e m i", m=MICRO, i=TPE)[:, :, :, t],
                                xa_bank[t][:, 0:D].rearrange("p (c e i) -> p c e i", c=DC, i=TPE),
                                attnb_sb[:].unsqueeze(2).unsqueeze(3).to_broadcast([P, DC, E, TPE]),
                                ALU.add).then_inc(xa_ready, 1)

            for n in range(NC):
                low_p(n)
            sum_rows(0)
            low_p(NC)
            divide_an(0)
            low_p(NC + 1)
            low_p(NC + 2)
            add_xattn(0)
            low_p(NC + 3)
            norm_x1(0)
            low_p(NC + 4)
            low_p(NC + 5)
            mean_squares(0)
            low_p(NC + 6)
            norm_qk(0)
            low_p(NC + 7)
            keep_k(0)
            sum_rows(1)
            top, shift = shift_scores(0)
            top(0)
            top(1)
            shift(0)
            shift(1)
            divide_an(1)
            divide_y(0)
            add_xattn(1)
            add_self(0)
            norm_x1(1)
            norm_x2(0)
            mean_squares(1)
            norm_h0(0)
            norm_qk(1)
            keep_k(1)
            keep_h0(0)
            top, shift = shift_scores(1)
            top(0)
            top(1)
            shift(0)
            shift(1)
            keep_xa(0)
            divide_y(1)
            add_self(1)
            norm_x2(1)
            norm_h0(1)
            keep_h0(1)
            keep_xa(1)

            def bias1(n):
                dve.wait_ge(f1_done, n + 1)
                V.tensor_tensor(wide_a[:, n], f1_bank[n], b1_sb[:, n // FH, (n % FH) * HALF:(n % FH + 1) * HALF],
                                ALU.add).then_inc(f1_biased, 1)

            def keep_h(n):
                dve.wait_ge(hT_done, n + 1)
                V.tensor_copy(wide_b[:, n], hT_bank[n]).then_inc(hT_ready, 1)

            def bias2(g):
                dve.wait_ge(f2_done, g + 1)
                V.tensor_tensor(h0[:, g], f2_bank[g][:, 0:D], b2_sb[:, g], ALU.add).then_inc(f2_ready, 1)

            def keep_y(g):
                dve.wait_ge(yT_done, g + 1)
                for m in range(MICRO):
                    dst = qT[:, m].rearrange("p c (e i) -> p c e i", i=TPE)[:, :, g * EG:(g + 1) * EG]
                    src = yT_bank[g][:, 0:D].rearrange("p (c e m i) -> p c e m i", c=DC, m=MICRO, i=TPE)
                    V.tensor_copy(dst, src[:, :, :, m]).then_inc(yT_ready, 1)

            dve.wait_ge(ld_late, 16 * N_LATE)
            bias1(0)
            bias1(1)
            keep_h(0)
            bias1(2)
            keep_h(1)
            bias1(3)
            keep_h(2)
            keep_h(3)
            bias2(0)
            keep_y(0)
            bias2(1)
            keep_y(1)
            for t in range(TT):
                dve.wait_ge(fin_done, t + 1)
                V.tensor_tensor(rows[:, t], fin_bank[t][:, 0:D], nextb_sb[:], ALU.add).then_inc(fin_biased, 1)
            for t in range(TT):
                dve.wait_ge(fin_gelu, t + 1)
                V.tensor_tensor(xres[:, t], xres[:, t], rows[:, t], ALU.add).then_inc(out_ready, 1)


_INS = ["x", "ctx_1024", "L0_xattn_Wq", "L0_xattn_bq", "L0_xattn_Wk", "L0_xattn_bk", "L0_xattn_Wv", "L0_xattn_bv",
        "L0_attn_w_qkv", "L0_attn_ln_w", "L0_attn_w_proj", "L0_ffn_ln_g", "L0_ffn_ln_b", "L0_ffn_attn_w",
        "L0_ffn_attn_b", "L0_ffn_w1", "L0_ffn_b1", "L0_ffn_w2", "L0_ffn_b2", "L0_ffn_next_w", "L0_ffn_next_b"]


def kernel(**inputs):
    import numpy as _np
    import concourse.bacc as _bacc
    from concourse import mybir as _mybir
    from concourse.bass_utils import run_bass_kernel_spmd as _run

    nc = _bacc.Bacc("TRN2", target_bir_lowering=False, num_devices=1)
    arrays, args = {}, []
    for name in _INS:
        a = _np.ascontiguousarray(inputs[name])
        arrays[f"in_{name}"] = a
        args.append(nc.dram_tensor(f"in_{name}", a.shape, _mybir.dt.from_np(a.dtype), kind="ExternalInput").ap())
    args.append(nc.dram_tensor("out_x", (1, 256, 256), _mybir.dt.float32, kind="ExternalOutput").ap())
    perceiver_block(nc, *args)
    r = _run(nc, [arrays], core_ids=[0])
    return r.results[0]["out_x"]
```

```python
from contextlib import ExitStack

import concourse.bass as bass
from concourse import mybir

F32 = mybir.dt.float32
F32R = mybir.dt.float32r
BF16 = mybir.dt.bfloat16
ACT = mybir.ActivationFunctionType
ALU = mybir.AluOpType
AX = mybir.AxisListType

P = 128
QUAD = 32


def perceiver_block(nc, x, ctx_in, xWq, xbq, xWk, xbk, xWv, xbv, w_qkv, ln_w, w_proj,
                    ln_g, ln_b, attn_w, attn_b, w1, b1, w2, b2, next_w, next_b, out):
    _, TOK, D = x.shape
    J = ctx_in.shape[1]
    E, _, DFF = w1.shape
    TT = TOK // P
    DC = D // P
    CHUNK = 512
    NC = J // CHUNK
    JB = CHUNK // P
    XSCALE = float(D) ** -0.5
    HEADS, LS = 16, 64
    HD = D // HEADS
    ASCALE = float(HD) ** -0.5
    GT = P // LS
    STRIPS = P // QUAD
    PAIRS = HEADS // 2
    VW = HD + 1
    MICRO = TT
    TPE = TOK // (MICRO * E)
    EG = P // (MICRO * TPE)
    EGN = E // EG
    HALF = 512
    FH = DFF // HALF
    FB = HALF // P
    LN_EPS, RMS_EPS = 1e-5, 1e-6
    MASKED = -1e38
    RAW_RING, T_RING, P_RING = 3, 2, 3
    W1_EARLY = 5
    SLOT = DC * DFF

    with ExitStack() as whole:
        def sem(name):
            return whole.enter_context(nc.semaphore(name))

        def sbuf(name, shape, dt=F32, stack=whole):
            return stack.enter_context(nc.sbuf_tensor(name, shape, dt))

        w1_early = sbuf("w1_early", [P, W1_EARLY, SLOT])
        wv_sb = sbuf("wv_sb", [P, DC, D])
        wqkv_sb = sbuf("wqkv_sb", [P, DC, 3 * D])
        wproj_sb = sbuf("wproj_sb", [P, DC, D])
        attnw_sb = sbuf("attnw_sb", [P, DC, D])
        nextw_sb = sbuf("nextw_sb", [P, DC, D])
        x_sb = sbuf("x_sb", [P, TT, D])
        xres = sbuf("xres", [P, TT, D])
        xaT = sbuf("xaT", [P, DC, TOK])
        bias_row = sbuf("bias_row", [P, D])
        nextb_sb = sbuf("nextb_sb", [1, D])
        ones_row = sbuf("ones_row", [1, P])
        ones_col = sbuf("ones_col", [P, 1])
        ident = sbuf("ident", [P, P])
        ident_bf = sbuf("ident_bf", [P, P], BF16)
        causal_bf = sbuf("causal_bf", [P, 4, LS], BF16)
        warm_bf = sbuf("warm_bf", [P, 512], BF16)
        mean_of = sbuf("mean_of", [P, P])
        shifted = sbuf("shifted", [P, GT, P])
        neg_half = sbuf("neg_half", [P, 1])
        strip_even = sbuf("strip_even", [P, STRIPS])
        parity = sbuf("parity", [P, 2])
        bq_sb = sbuf("bq_sb", [P, DC])
        bk_sb = sbuf("bk_sb", [P, DC])
        lnw_sb = sbuf("lnw_sb", [P, DC])
        lnw_par = sbuf("lnw_par", [P, DC, 2])
        lng_sb = sbuf("lng_sb", [P, DC])
        lnb_sb = sbuf("lnb_sb", [P, DC])
        attnb_sb = sbuf("attnb_sb", [P, DC])
        bn6 = sbuf("bn6", [P, TT, 6])
        mv = sbuf("mv", [P, TT, 2])
        mean_sq = sbuf("mean_sq", [P, TT, 2])
        rms_eps = sbuf("rms_eps", [P, TT])
        base = sbuf("base", [P, TT, 5])
        root = sbuf("root", [P, TT, 5])
        row_max = sbuf("row_max", [P, TT])
        inv_sum = sbuf("inv_sum", [P, TT])
        head_max = sbuf("head_max", [P, TT, STRIPS, 4])
        inv_den = sbuf("inv_den", [P, TT, HEADS])
        table_junk = sbuf("table_junk", [P, 1])

        with ExitStack() as early:
            cH = sbuf("cH", [P, NC, JB, D + 2], F32R, early)
            cL = sbuf("cL", [P, NC, JB, D], F32R, early)
            scores1 = sbuf("scores1", [P, NC, CHUNK], F32, early)
            pH = sbuf("pH", [P, P_RING, CHUNK], F32R, early)
            pL = sbuf("pL", [P, P_RING, CHUNK], F32R, early)
            scores0 = sbuf("scores0", [P, NC, CHUNK], F32, early)
            tH = sbuf("tH", [P, T_RING, DC, CHUNK], F32R, early)
            tL = sbuf("tL", [P, T_RING, DC, CHUNK], F32R, early)
            raw = sbuf("raw_ctx", [P, RAW_RING, JB, D], F32, early)
            gH = sbuf("gH", [P, DC, TOK], F32R, early)
            gL = sbuf("gL", [P, DC, TOK], F32R, early)
        with ExitStack() as late:
            over_cH = sbuf("over_cH", [P, 4, SLOT], F32, late)
            sbuf("rest_of_cH", [P, 2 * NC * JB], F32, late)
            over_cL = sbuf("over_cL", [P, 4, SLOT], F32, late)
            over_scores1 = sbuf("over_scores1", [P, 2, SLOT], F32, late)
            over_p = sbuf("over_p", [P, 2 * P_RING * CHUNK], F32, late)
            b1_sb = sbuf("b1_sb", [P, EGN, DFF], F32, late)
            b2_sb = sbuf("b2_sb", [P, EGN, D], F32, late)
            h0 = sbuf("h0", [P, TT, D], F32, late)
            sbuf("rest_of_scores0", [P, NC * CHUNK - EGN * DFF - EGN * D - TT * D], F32, late)
            wide_a = sbuf("wide_a", [P, 4, 512], F32, late)
            wide_b = sbuf("wide_b", [P, 4, 512], F32, late)
            v2 = sbuf("v2", [P, TT, GT, PAIRS, 2, VW], F32, late)
            rows = sbuf("rows", [P, TT, D], F32, late)
            cols = sbuf("cols", [P, TT, DC, P], F32, late)
            qT = sbuf("qT", [P, TT, DC, P], F32, late)
            kT = sbuf("kT", [P, TT, DC, 2, P], F32, late)

        scores = [scores0, scores1]
        top = xaT[:].rearrange("p a b -> p (a b)").rearrange("p (t b i) -> p t b i", t=TT, b=2)
        shift_row = wide_a[:, 3, 0:TT * P].rearrange("p (t i) -> p t i", t=TT)
        pre = scores1[:].rearrange("p k j -> p (k j)")

        def prelude(n):
            return pre[:, (n + 1) * 512:(n + 2) * 512].rearrange("p (a b) -> p a b", a=2)
        xn, wq_sb, wk_sb, wkT, xnT, xqT = (prelude(n) for n in range(6))

        spare = wide_b[:].rearrange("p a b -> p (a b)").rearrange("p (t s d) -> p t s d", t=TT, s=4)

        places = [(over_cH[:, 0], 2), (over_cL[:, 0], 2), (over_cH[:, 1], 4), (over_cL[:, 1], 4),
                  (over_scores1[:, 0], 4), (over_cH[:, 2], 6), (over_cL[:, 2], 6), (over_cH[:, 3], 8),
                  (over_cL[:, 3], 8), (over_scores1[:, 1], 8), (over_p[:, 0:SLOT], 8)]
        W1_LATE = E - W1_EARLY

        def w1_of(e):
            return w1_early[:, e] if e < W1_EARLY else places[e - W1_EARLY][0]

        def w2_of(e):
            return places[W1_LATE + e][0].rearrange("p (h b d) -> p h b d", h=FH, b=FB)

        psum = whole.enter_context(nc.psum_tensor("psum", [P, 8, 512], F32))
        bank = [psum[:, n] for n in range(8)]
        A_bank = bank[6:8]

        def s_bank(k, h):
            return bank[2 + 2 * (k % 2) + h]

        an_bank, xo_bank, x1_bank = [bank[2], bank[0]], [bank[3], bank[1]], [bank[4], bank[0]]
        q_bank, k_bank, v_bank = [bank[5], bank[1]], [bank[3], bank[7]], [bank[2], bank[6]]
        qT_bank, kT_bank = [bank[5], bank[7]], [bank[6], bank[3]]
        a_first = [3, 0]
        at_bank = [[bank[2], bank[3]], [bank[7], bank[0]]]
        y_bank, yn_bank, proj_bank = [bank[4], bank[1]], [bank[5], bank[2]], [bank[4], bank[3]]
        x2_bank, xa_bank, xaT_bank = [bank[5], bank[2]], [bank[4], bank[3]], [bank[5], bank[2]]
        f1_bank = [bank[4], bank[7], bank[0], bank[1]]
        hT_bank = [bank[2], bank[5], bank[4], bank[7]]
        f2_bank, yT_bank, fin_bank = [bank[6], bank[3]], [bank[0], bank[1]], [bank[2], bank[5]]

        ld_x, ld_wk, ld_wq, ld_bq, ld_bk, ld_bv, ld_small, ld_rest, ld_nextb, ld_late, stored = (
            sem(n) for n in ("ld_x", "ld_wk", "ld_wq", "ld_bq", "ld_bk", "ld_bv", "ld_small", "ld_rest", "ld_nextb", "ld_late", "stored"))
        ld_ctx = [sem(f"ld_ctx{k}") for k in range(NC)]
        ld_w1 = [sem(f"ld_w1_{e}") for e in range(E)]
        ld_w2 = [sem(f"ld_w2_{e}") for e in range(E)]
        consts = sem("consts")
        warm_ready, xbv_ready, idbf_ready, lnw_ready, shifted_ready = (
            sem(n) for n in ("warm_ready", "xbv_ready", "idbf_ready", "lnw_ready", "shifted_ready"))
        var_ready = [sem(f"var_ready{t}") for t in range(TT)]
        root_ready = [sem(f"root_ready{t}") for t in range(TT)]
        xn_ready, x1_ready, x2_ready, dve_order, act_order = (
            sem(n) for n in ("xn_ready", "x1_ready", "x2_ready", "dve_order", "act_order"))
        wkT_done, wkT_ready, xnT_done, xnT_ready = (
            sem(n) for n in ("wkT_done", "wkT_ready", "xnT_done", "xnT_ready"))
        q_done, q_ready, g_done, qbk_done = (sem(n) for n in ("q_done", "q_ready", "g_done", "qbk_done"))
        attn_bias_done, attnw_scaled, attnw_mean_done, attnw_centred, qkv_mean_done, qkv_centred = (
            sem(n) for n in ("attn_bias_done", "attnw_scaled", "attnw_mean_done", "attnw_centred",
                             "qkv_mean_done", "qkv_centred"))
        gH_ready, gL_ready = sem("gH_ready"), sem("gL_ready")
        t_done, tH_ready, tL_ready = sem("t_done"), sem("tH_ready"), sem("tL_ready")
        s_done, s_ready, top_ready, topT_done, row_max_ready, max_row_done, shift_row_ready = (
            sem(n) for n in ("s_done", "s_ready", "top_ready", "topT_done", "row_max_ready", "max_row_done",
                             "shift_row_ready"))
        cH_ready, cL_ready = sem("cH_ready"), sem("cL_ready")
        pL_first_ready = sem("pL_first_ready")
        s_shifted, p_ready, pH_ready, pL_ready, pv_done, ones_col_ready, qbk_ready = (
            sem(n) for n in ("s_shifted", "p_ready", "pH_ready", "pL_ready", "pv_done", "ones_col_ready", "qbk_ready"))
        an_ready, anT_done, anT_ready, xo_done, x1T_done, x1T_ready = (
            sem(n) for n in ("an_ready", "anT_done", "anT_ready", "xo_done", "x1T_done", "x1T_ready"))
        qk_rows_done, v_rows_done, v_rows_ready, v_done, v_ready, ones_ready = (
            sem(n) for n in ("qk_rows_done", "v_rows_done", "v_rows_ready", "v_done", "v_ready", "ones_ready"))
        sq_ready, qn_ready, kn_ready, qT_done, kT_done, qT_ready, kT_ready = (
            sem(n) for n in ("sq_ready", "qn_ready", "kn_ready", "qT_done", "kT_done", "qT_ready", "kT_ready"))
        a_done, a_max, a_shifted, a_exp, at_done, at_ready = (
            sem(n) for n in ("a_done", "a_max", "a_shifted", "a_exp", "at_done", "at_ready"))
        y_done, yn_ready, ynT_done, ynT_ready, proj_done = (
            sem(n) for n in ("y_done", "yn_ready", "ynT_done", "ynT_ready", "proj_done"))
        x2T_done, x2T_ready, xa_done, xa_rows_ready, xaT_done, xaT_ready = (
            sem(n) for n in ("x2T_done", "x2T_ready", "xa_done", "xa_rows_ready", "xaT_done", "xaT_ready"))
        f1_done, f1_biased, gelu_ready, hT_done, hT_ready, f2_done, f2_ready = (
            sem(n) for n in ("f1_done", "f1_biased", "gelu_ready", "hT_done", "hT_ready", "f2_done", "f2_ready"))
        yT_done, yT_ready, fin_done, fin_gelu, out_ready = (
            sem(n) for n in ("yT_done", "yT_ready", "fin_done", "fin_gelu", "out_ready"))

        DVE_LOW = 2
        N_REST, N_SMALL, N_LATE = 5, 4, 2 * EGN

        block = whole.enter_context(nc.Block())

        def halves(w):
            return w.rearrange("(c p) n -> p c n", p=P)

        def per_partition(v):
            return v.rearrange("(c p) -> p c", p=P)

        def row(v):
            return v.rearrange("(a n) -> a n", a=1)

        @block.sync
        def _(sp):
            def load_ctx(k):
                if k >= RAW_RING:
                    sp.wait_ge(t_done, DC * (k - RAW_RING + 1))
                    sp.wait_ge(cH_ready, k - RAW_RING + 1)
                    sp.wait_ge(cL_ready, k - RAW_RING + 1)
                src = ctx_in[0, k * CHUNK:(k + 1) * CHUNK, :].rearrange("(p b) d -> p (b d)", b=JB)
                sp.dma_start(raw[:, k % RAW_RING].rearrange("p b d -> p (b d)"), src).then_inc(ld_ctx[k], 16)

            def load_w1(e):
                sp.dma_start(w1_of(e), w1[e].rearrange("(p c) f -> p (c f)", c=DC)).then_inc(ld_w1[e], 16)

            sp.dma_start(x_sb[:], x[0].rearrange("(t p) d -> p t d", p=P)).then_inc(ld_x, 16)
            sp.dma_start(wk_sb, halves(xWk)).then_inc(ld_wk, 16)
            for k in range(RAW_RING):
                load_ctx(k)
            for dst, src in ((wv_sb, xWv), (wqkv_sb, w_qkv), (wproj_sb, w_proj), (attnw_sb, attn_w),
                             (nextw_sb, next_w)):
                sp.dma_start(dst[:], halves(src)).then_inc(ld_rest, 16)
            sp.dma_start(bias_row[:], row(xbv).to_broadcast([P, D])).then_inc(ld_bv, 16)
            for dst, src in ((lnw_sb, ln_w), (lng_sb, ln_g), (lnb_sb, ln_b)):
                sp.dma_start(dst[:], per_partition(src), allow_slow_non_contiguous=True).then_inc(ld_small, 16)
            sp.dma_start(attnb_sb[:], attn_b.rearrange("(p c) -> p c", c=DC)).then_inc(ld_small, 16)
            sp.dma_start(nextb_sb[:], row(next_b)).then_inc(ld_nextb, 16)
            for k in range(RAW_RING, NC):
                load_ctx(k)
                if k < NC - 2:
                    load_w1(k - RAW_RING)
            for e in range(NC - 2 - RAW_RING, W1_EARLY):
                load_w1(e)
            sp.wait_ge(pL_ready, NC - DVE_LOW)
            sp.wait_ge(pL_first_ready, DVE_LOW)
            for g in range(EGN):
                for dst, src in ((b1_sb, b1), (b2_sb, b2)):
                    width = src.shape[-1]
                    sp.dma_start(dst[:, g], src[g * EG:(g + 1) * EG, :].unsqueeze(1).to_broadcast([EG, QUAD, width])
                                 ).then_inc(ld_late, 16)
            for n, (_, used) in enumerate(places):
                sp.wait_ge(pv_done, NC + used)
                if n < W1_LATE:
                    load_w1(W1_EARLY + n)
                else:
                    e = n - W1_LATE
                    sp.dma_start(w2_of(e), w2[e].rearrange("(h p b) d -> p h b d", h=FH, b=FB)).then_inc(ld_w2[e], 16)
            for t in range(TT):
                sp.wait_ge(out_ready, t + 1)
                sp.dma_start(out[0, t * P:(t + 1) * P, :], xres[:, t, :]).then_inc(stored, 16)
            sp.wait_ge(stored, 16 * TT)

        @block.gpsimd
        def _(pool):
            nc.gpsimd.memset(ident[:], 0.0).then_inc(consts, 1)
            nc.gpsimd.memset(neg_half[:], -0.5).then_inc(consts, 1)
            pool.dma_start(bq_sb[:], per_partition(xbq), allow_slow_non_contiguous=True).then_inc(ld_bq, 16)
            pool.dma_start(bk_sb[:], per_partition(xbk), allow_slow_non_contiguous=True).then_inc(ld_bk, 16)
            pool.wait_ge(consts, 2)
            nc.gpsimd.affine_select(out=ident[:], in_=ident[:], compare_op=ALU.not_equal, fill=1.0, base=0,
                                    pattern=[[-1, P]], channel_multiplier=1).then_inc(consts, 1)

            powers = [0, 0]

            def power(t, which):
                powers[t] += 1
                pool.wait_ge(var_ready[t], powers[t])
                nc.gpsimd.tensor_tensor(root[:, t, which:which + 1], base[:, t, which:which + 1], neg_half[:],
                                        ALU.pow).then_inc(root_ready[t], 1)
            power(0, 0)
            power(1, 0)

            def low_rows(k):
                pool.wait_ge(cH_ready, k + 1)
                nc.gpsimd.tensor_tensor(cL[:, k], raw[:, k % RAW_RING], cH[:, k, :, 0:D].bitcast(F32),
                                        ALU.subtract).then_inc(cL_ready, 1)

            low_rows(0)
            low_rows(1)
            nc.gpsimd.memset(causal_bf[:], 0.0).then_inc(consts, 1)
            nc.gpsimd.memset(strip_even[:], 1.0).then_inc(consts, 1)
            for g in range(2):
                pool.wait_ge(consts, 5 + g)
                part = causal_bf[g * LS:(g + 1) * LS]
                nc.gpsimd.affine_select(out=part, in_=part, compare_op=ALU.is_ge, fill=MASKED, base=0,
                                        pattern=[[0, 4], [-1, LS]], channel_multiplier=1).then_inc(consts, 1)
            pool.wait_ge(consts, 7)
            nc.gpsimd.affine_select(out=strip_even[:], in_=strip_even[:], compare_op=ALU.is_ge, fill=0.0, base=0,
                                    pattern=[[-QUAD, STRIPS]], channel_multiplier=1).then_inc(consts, 1)
            pool.wait_ge(consts, 8)
            nc.gpsimd.affine_select(out=strip_even[:], in_=strip_even[:], compare_op=ALU.is_ge, fill=0.0, base=HD - 1,
                                    pattern=[[QUAD, STRIPS]], channel_multiplier=-1).then_inc(consts, 1)
            pool.wait_ge(ld_bv, 16)
            for t in range(TT):
                nc.gpsimd.tensor_tensor(xres[:, t], x_sb[:, t], bias_row[:], ALU.add).then_inc(xbv_ready, 1)
            for k in range(2, NC):
                low_rows(k)
            pool.wait_ge(s_done, TT * NC)
            pool.wait_ge(cL_ready, NC)
            nc.gpsimd.memset(v2[:], 0.0).then_inc(ones_ready, 1)
            pool.wait_ge(ones_ready, 1)
            for par in range(2):
                nc.gpsimd.memset(v2[par * LS:(par + 1) * LS, :, :, :, par, HD], 1.0).then_inc(ones_ready, 1)
                pool.wait_ge(ones_ready, 2 + par)

            def low_p(n):
                t, k = divmod(n, NC)
                pool.wait_ge(pH_ready, n + 1)
                nc.gpsimd.tensor_tensor(pL[:, n % P_RING], scores[t][:, k], pH[:, n % P_RING].bitcast(F32),
                                        ALU.subtract).then_inc(pL_ready, 1)

            for n in range(DVE_LOW, NC):
                low_p(n)
            low_p(8)
            low_p(9)
            low_p(10)
            low_p(11)
            power(0, 0)
            low_p(12)
            power(0, 1)
            power(0, 2)
            low_p(13)
            low_p(14)
            low_p(15)
            power(1, 0)
            power(1, 1)
            power(1, 2)
            power(0, 3)
            power(0, 4)
            power(1, 3)
            power(1, 4)

        @block.tensor
        def _(pe):
            mm = nc.tensor.matmul

            def transpose(dst, src):
                return nc.tensor.transpose(dst, src, ident[:])

            def warm(dst, n):
                for _ in range(n):
                    mm(dst, warm_bf[:, 0:P], warm_bf[:], start=True, stop=True)

            pe.wait_ge(warm_ready, 1)
            warm(bank[5], 9)
            pe.wait_ge(consts, 3)

            for t in range(TT):
                pe.wait_ge(xn_ready, t + 1)
                for c in range(DC):
                    last = transpose(bank[6 + t][:, c * P:(c + 1) * P], xn[:, t, c * P:(c + 1) * P])
                last.then_inc(xnT_done, 1)

            def turn_ctx(k):
                pe.wait_ge(ld_ctx[k], 16)
                for c in range(DC):
                    if k >= 1:
                        pe.wait_ge(tL_ready, DC * (k - 1) + c + 1)
                    for b in range(JB):
                        last = transpose(bank[c][:, b * P:(b + 1) * P], raw[:, k % RAW_RING, b, c * P:(c + 1) * P])
                    last.then_inc(t_done, 1)

            turn_ctx(0)
            pe.wait_ge(ld_wq, 16)
            pe.wait_ge(xnT_ready, TT)
            for e in range(DC):
                for c in range(DC):
                    last = mm(bank[2 + e][:, 0:TOK], wq_sb[:, c, e * P:(e + 1) * P], xnT[:, c],
                              start=(c == 0), stop=(c == DC - 1))
                last.then_inc(q_done, 1)
            pe.wait_ge(ld_wk, 16)
            for e in range(DC):
                for d in range(DC):
                    last = transpose(bank[6][:, e * D + d * P:e * D + (d + 1) * P], wk_sb[:, d, e * P:(e + 1) * P])
            last.then_inc(wkT_done, 1)
            turn_ctx(1)
            pe.wait_ge(wkT_ready, 1)
            pe.wait_ge(q_ready, DC)
            for d in range(DC):
                for e in range(DC):
                    last = mm(bank[4 + d][:, 0:TOK], wkT[:, e, d * P:(d + 1) * P], xqT[:, e],
                              start=(e == 0), stop=(e == DC - 1))
                last.then_inc(g_done, 1)

            def bias_scores():
                pe.wait_ge(ld_bk, 16)
                for e in range(DC):
                    last = mm(bank[7][:, 0:TOK], bk_sb[:, e:e + 1].to_broadcast([P, P]), xqT[:, e],
                              start=(e == 0), stop=(e == DC - 1))
                last.then_inc(qbk_done, 1)

            for k in range(NC):
                if 1 <= k < NC - 1:
                    turn_ctx(k + 1)
                for h in range(2):
                    if k >= 2:
                        pe.wait_ge(s_ready, 2 * TT * (k - 2) + TT * (h + 1))
                    elif k == 1:
                        pe.wait_ge(gL_ready, DC)
                    for c in range(DC):
                        for b in (2 * h, 2 * h + 1):
                            dst = s_bank(k, h)[:, (b % 2) * TOK:(b % 2 + 1) * TOK]
                            at = slice(b * P, (b + 1) * P)
                            pe.wait_ge(gH_ready, c + 1)
                            pe.wait_ge(tH_ready, DC * k + c + 1)
                            mm(dst, tH[:, k % T_RING, c, at], gH[:, c], start=(c == 0 and b == 2 * h), stop=False,
                               skip_group_check=True)
                            pe.wait_ge(tL_ready, DC * k + c + 1)
                            mm(dst, tL[:, k % T_RING, c, at], gH[:, c], start=False, stop=False,
                               skip_group_check=True)
                            pe.wait_ge(gL_ready, c + 1)
                            last = mm(dst, tH[:, k % T_RING, c, at], gL[:, c], start=False, stop=(c == DC - 1),
                                      skip_group_check=True)
                    last.then_inc(s_done, 1)
                    if k == 0 and h == 0:
                        bias_scores()
                if k == 3:
                    pe.wait_ge(ld_rest, 16 * N_REST)
                    pe.wait_ge(ld_small, 16 * N_SMALL)
                    for dc in range(DC):
                        for c in range(DC):
                            last = mm(bank[6][:, dc:dc + 1], attnw_sb[:, c, dc:D:DC], lnb_sb[:, c:c + 1],
                                      start=(c == 0), stop=(c == DC - 1))
                    last.then_inc(attn_bias_done, 1)

            pe.wait_ge(warm_ready, 3)
            pe.wait_ge(s_ready, 2 * TT * (NC - 1))

            def qkv_mean(dst, lo, hi, c):
                return mm(dst, mean_of[:], wqkv_sb[:, c, lo:hi], start=(c == 0), stop=(c == DC - 1))
            qkv_mean(bank[2], 0, 2 * D, 0)
            for t in range(TT):
                pe.wait_ge(top_ready, 2 * NC * TT - (TT - 1 - t))
                for b in range(2):
                    last = transpose(bank[t][:, b * P:(b + 1) * P], top[:, t, b])
                last.then_inc(topT_done, 1)
            qkv_mean(bank[3][:, 0:D], 2 * D, 3 * D, 0)
            for t in range(TT):
                pe.wait_ge(row_max_ready, t + 1)
                mm(bank[4 + t][:, 0:P], row_max[:, t:t + 1].to_broadcast([P, P]), ident[:], start=True,
                   stop=True).then_inc(max_row_done, 1)
            qkv_mean(bank[2], 0, 2 * D, 1)
            qkv_mean(bank[3][:, 0:D], 2 * D, 3 * D, 1).then_inc(qkv_mean_done, 1)

            def attn_mean():
                pe.wait_ge(attnw_scaled, DC + 1)
                for c in range(DC):
                    last = mm(bank[7][:, 0:D], mean_of[:], attnw_sb[:, c], start=(c == 0), stop=(c == DC - 1))
                last.then_inc(attnw_mean_done, 1)

            def weigh(n, half):
                t, k = divmod(n, NC)
                if half == 0:
                    pe.wait_ge(pH_ready, n + 1)
                    pe.wait_ge(cL_ready, k + 1)
                    pe.wait_ge(ones_col_ready, 1)
                    if n == NC:
                        pe.wait_ge(attnw_centred, DC)
                for left, right in ((pH, cH), (pH, cL), (pL, cH)):
                    if half == 0 and left is pL:
                        if n < DVE_LOW:
                            pe.wait_ge(pL_first_ready, n + 1)
                        else:
                            pe.wait_ge(pL_ready, n - DVE_LOW + 1)
                    width = D + 2 if right is cH else D
                    for b in range(half * JB // 2, (half + 1) * JB // 2):
                        last = mm(A_bank[t][:, 0:width], left[:, n % P_RING, b * P:(b + 1) * P], right[:, k, b, 0:width],
                                  start=(k == 0 and b == 0 and left is pH and right is cH),
                                  stop=(k == NC - 1 and b == JB - 1 and left is pL))
                if half:
                    last.then_inc(pv_done, 1)

            def turn_rows(t, dst, src, ready, done):
                pe.wait_ge(ready, t + 1)
                for c in range(DC):
                    last = transpose(dst[:, c * P:(c + 1) * P], src[:, c * P:(c + 1) * P])
                last.then_inc(done, 1)

            def turn_an(t):
                turn_rows(t, an_bank[t], rows[:, t], an_ready, anT_done)

            def xattn_out(t):
                pe.wait_ge(anT_ready, t + 1)
                for c in range(DC):
                    last = mm(xo_bank[t][:, 0:D], cols[:, t, c], wv_sb[:, c], start=(c == 0), stop=(c == DC - 1))
                last.then_inc(xo_done, 1)

            def turn_x1(t):
                turn_rows(t, x1_bank[t], x_sb[:, t], x1_ready, x1T_done)

            def project_qk(t):
                pe.wait_ge(x1T_ready, t + 1)
                pe.wait_ge(qkv_centred, 2 * DC)
                for s, rows_bank in enumerate((q_bank[t], k_bank[t])):
                    for c in range(DC):
                        last = mm(rows_bank[:, 0:D], cols[:, t, c], wqkv_sb[:, c, s * D:(s + 1) * D],
                                  start=(c == 0), stop=(c == DC - 1))
                    last.then_inc(qk_rows_done, 1)

            def project_v(t):
                for c in range(DC):
                    last = mm(v_bank[t][:, 0:D], cols[:, t, c], wqkv_sb[:, c, 2 * D:3 * D],
                              start=(c == 0), stop=(c == DC - 1))
                last.then_inc(v_rows_done, 1)

            def shift_v(t):
                pe.wait_ge(v_rows_ready, t + 1)
                pe.wait_ge(shifted_ready, GT)
                for g in range(GT):
                    last = mm(v_bank[t][:, g * D:(g + 1) * D], shifted[:, g], spare[:, t, 3], start=True, stop=True)
                last.then_inc(v_done, 1)

            def turn_qk(t):
                for s, dst, ready, done in ((1, kT_bank[t], kn_ready, kT_done), (0, qT_bank[t], qn_ready, qT_done)):
                    pe.wait_ge(ready, t + 1)
                    for c in range(DC):
                        last = transpose(dst[:, c * P:(c + 1) * P], spare[:, t, s, c * P:(c + 1) * P])
                    last.then_inc(done, 1)

            def self_scores(t):
                pe.wait_ge(idbf_ready, 1)
                for h in range(2):
                    for i in (2 * h, 2 * h + 1):
                        mm(bank[a_first[t] + i][:, 0:4 * LS], ident_bf[:], causal_bf[:].rearrange("p a k -> p (a k)"),
                           start=True, stop=False, skip_group_check=True)
                    pe.wait_ge(kT_ready, t + 1)
                    pe.wait_ge(qT_ready, DC * (t + 1))
                    for c in range(DC):
                        for i in (2 * h, 2 * h + 1):
                            strip = slice(i * QUAD, (i + 1) * QUAD)
                            for g in range(GT):
                                tok = slice(g * LS, (g + 1) * LS)
                                last = mm(bank[a_first[t] + i][tok, c * 2 * LS:(c + 1) * 2 * LS], qT[strip, t, c, tok],
                                          kT[strip, t, c, :, tok], start=False, stop=True, skip_group_check=True)
                    last.then_inc(a_done, 1)

            def turn_a(t, h):
                pe.wait_ge(a_exp, 2 * t + h + 1)
                if t == 0:
                    pe.wait_ge(v_ready, 2)
                for i in range(2):
                    for c in range(DC):
                        at = (i * DC + c) * P
                        last = transpose(at_bank[t][h][:, at:at + P], wide_a[:, 2 * t + h, at:at + P])
                last.then_inc(at_done, 1)

            def self_values(t, h):
                pe.wait_ge(at_ready, 2 * t + h + 1)
                pe.wait_ge(v_ready, 2 * (t + 1))
                for i in range(2):
                    for c in range(DC):
                        pair = c * STRIPS + 2 * h + i
                        for g in range(GT):
                            at = (i * DC + c) * P + g * LS
                            last = mm(y_bank[t][g * LS:(g + 1) * LS, pair * 2 * VW:(pair + 1) * 2 * VW],
                                      wide_b[:, 2 * t + h, at:at + LS],
                                      v2[:, t, g, pair].rearrange("p r e -> p (r e)"), start=True, stop=True)
                if h:
                    last.then_inc(y_done, 1)

            def turn_yn(t):
                turn_rows(t, yn_bank[t], rows[:, t], yn_ready, ynT_done)

            def project_y(t):
                pe.wait_ge(ynT_ready, t + 1)
                for c in range(DC):
                    last = mm(proj_bank[t][:, 0:D], cols[:, t, c], wproj_sb[:, c], start=(c == 0), stop=(c == DC - 1))
                last.then_inc(proj_done, 1)

            def turn_x2(t):
                turn_rows(t, x2_bank[t], xres[:, t], x2_ready, x2T_done)

            def x_attn(t):
                pe.wait_ge(x2T_ready, t + 1)
                for c in range(DC):
                    last = mm(xa_bank[t][:, 0:D], cols[:, t, c], attnw_sb[:, c], start=(c == 0), stop=(c == DC - 1))
                last.then_inc(xa_done, 1)

            def turn_xa(t):
                pe.wait_ge(xa_rows_ready, t + 1)
                for dc in range(DC):
                    last = transpose(xaT_bank[t][:, dc * P:(dc + 1) * P], rows[:, t, dc:D:DC])
                last.then_inc(xaT_done, 1)

            attn_mean()
            for k in range(NC):
                weigh(k, 0)
                weigh(k, 1)
            for k in range(NC):
                n = NC + k
                weigh(n, 0)
                if k == 0:
                    turn_an(0)
                if k == 1:
                    xattn_out(0)
                if k == 3:
                    project_qk(0)
                    project_v(0)
                if k == 7:
                    turn_a(0, 0)
                weigh(n, 1)
                if k == 1:
                    turn_x1(0)
                if k == 4:
                    turn_qk(0)
                if k == 5:
                    self_scores(0)
                    shift_v(0)
                if k == 7:
                    turn_a(0, 1)
                    self_values(0, 0)
            turn_an(1)
            self_values(0, 1)
            xattn_out(1)
            warm(bank[5], 2)
            turn_x1(1)
            turn_yn(0)
            warm(bank[4], 2)
            project_qk(1)
            project_v(1)
            project_y(0)
            turn_qk(1)
            warm(bank[5], 2)
            self_scores(1)
            turn_x2(0)
            shift_v(1)
            turn_a(1, 0)
            x_attn(0)
            turn_a(1, 1)
            self_values(1, 0)
            self_values(1, 1)
            turn_xa(0)
            warm(bank[4], 3)
            turn_yn(1)
            warm(bank[4], 3)
            project_y(1)
            warm(bank[4], 3)
            turn_x2(1)
            warm(bank[4], 2)
            x_attn(1)
            warm(bank[4], 4)
            turn_xa(1)

            def first(g, h):
                n = g * FH + h
                if n == 0:
                    pe.wait_ge(xaT_ready, TT)
                for dc in range(DC):
                    for j in range(EG):
                        e = g * EG + j
                        if h == 0 and dc == 0:
                            pe.wait_ge(ld_w1[e], 16)
                        last = mm(f1_bank[n][j * QUAD:(j + 1) * QUAD, :], xaT[:, dc, e * QUAD:(e + 1) * QUAD],
                                  w1_of(e)[:, dc * DFF + h * HALF:dc * DFF + (h + 1) * HALF],
                                  start=(dc == 0), stop=(dc == DC - 1))
                last.then_inc(f1_done, 1)

            def turn_h(g, h):
                n = g * FH + h
                pe.wait_ge(gelu_ready, n + 1)
                for b in range(FB):
                    last = transpose(hT_bank[n][:, b * P:(b + 1) * P], wide_a[:, n, b:HALF:FB])
                last.then_inc(hT_done, 1)

            def second(g, h):
                n = g * FH + h
                pe.wait_ge(hT_ready, n + 1)
                for b in range(FB):
                    for j in range(EG):
                        e = g * EG + j
                        if b == 0 and h == 0:
                            pe.wait_ge(ld_w2[e], 16)
                        last = mm(f2_bank[g][j * QUAD:(j + 1) * QUAD, 0:D],
                                  wide_b[:, n, b * P + j * QUAD:b * P + (j + 1) * QUAD], w2_of(e)[:, h, b],
                                  start=(h == 0 and b == 0), stop=(h == FH - 1 and b == FB - 1))
                if h == FH - 1:
                    last.then_inc(f2_done, 1)

            def turn_y(g):
                pe.wait_ge(f2_ready, g + 1)
                for c in range(DC):
                    last = transpose(yT_bank[g][:, c * P:(c + 1) * P], h0[:, g, c * P:(c + 1) * P])
                last.then_inc(yT_done, 1)

            def next_bias(t):
                pe.wait_ge(ld_nextb, 16)
                mm(fin_bank[t][:, 0:D], ones_row[0:1, :], nextb_sb[0:1, :], start=True, stop=False)

            first(0, 0)
            first(0, 1)
            turn_h(0, 0)
            first(1, 0)
            turn_h(0, 1)
            first(1, 1)
            second(0, 0)
            turn_h(1, 0)
            second(0, 1)
            turn_h(1, 1)
            second(1, 0)
            turn_y(0)
            second(1, 1)
            next_bias(0)
            turn_y(1)
            next_bias(1)
            for t in range(TT):
                pe.wait_ge(yT_ready, MICRO * (EGN - 1) + t + 1)
                for c in range(DC):
                    last = mm(fin_bank[t][:, 0:D], qT[:, t, c], nextw_sb[:, c], start=False, stop=(c == DC - 1))
                last.then_inc(fin_done, 1)

        @block.scalar
        def _(act):
            A = nc.scalar.activation
            act.dma_start(wq_sb, halves(xWq)).then_inc(ld_wq, 16)
            act.wait_ge(warm_ready, 1)
            A(table_junk[:], warm_bf[:, 0:1], ACT.Exp).then_inc(act_order, 1)

            def high_ctx(k):
                for c in range(DC):
                    act.wait_ge(t_done, DC * k + c + 1)
                    if k >= T_RING and c == 0:
                        act.wait_ge(s_done, 2 * (k - T_RING + 1))
                    A(tH[:, k % T_RING, c], bank[c], ACT.Copy).then_inc(tH_ready, 1)

            def high_rows(k):
                act.wait_ge(ld_ctx[k], 16)
                A(cH[:, k, :, 0:D], raw[:, k % RAW_RING], ACT.Copy).then_inc(cH_ready, 1)

            high_ctx(0)
            high_rows(0)
            act.wait_ge(wkT_done, 1)
            A(wkT, bank[6].rearrange("p (a b) -> p a b", a=2), ACT.Copy).then_inc(wkT_ready, 1)
            high_rows(1)
            for d in range(DC):
                act.wait_ge(g_done, d + 1)
                A(gH[:, d], bank[4 + d][:, 0:TOK], ACT.Copy).then_inc(gH_ready, 1)
            high_ctx(1)

            def keep_scores(k, h):
                act.wait_ge(s_done, 2 * k + h + 1)
                src = s_bank(k, h).rearrange("p (b t i) -> p b t i", b=2, t=TT)
                for t in range(TT):
                    A(scores[t][:, k].rearrange("p (b i) -> p b i", b=JB)[:, 2 * h:2 * h + 2], src[:, :, t],
                      ACT.Copy).then_inc(s_ready, 1)

            for k in range(NC):
                if 1 <= k < NC - 1:
                    high_ctx(k + 1)
                keep_scores(k, 0)
                if 1 <= k < NC - 1:
                    high_rows(k + 1)
                keep_scores(k, 1)

            def exps(n):
                t, k = divmod(n, NC)
                act.wait_ge(s_shifted, n + 1)
                A(scores[t][:, k], scores[t][:, k], ACT.Exp, scale=XSCALE).then_inc(p_ready, 1)

            def high_p(n):
                t, k = divmod(n, NC)
                act.wait_ge(p_ready, n + 1)
                if n >= P_RING:
                    act.wait_ge(pv_done, n - P_RING + 1)
                A(pH[:, n % P_RING], scores[t][:, k], ACT.Copy).then_inc(pH_ready, 1)

            def keep_cols(t, src, done, ready):
                act.wait_ge(done, t + 1)
                A(cols[:, t], src[:, 0:D].rearrange("p (c i) -> p c i", c=DC), ACT.Copy).then_inc(ready, 1)

            def keep_an(t):
                keep_cols(t, an_bank[t], anT_done, anT_ready)

            def keep_x1(t):
                keep_cols(t, x1_bank[t], x1T_done, x1T_ready)

            def squares(t):
                for s, rows_bank in enumerate((q_bank[t], k_bank[t])):
                    act.wait_ge(qk_rows_done, 2 * t + s + 1)
                    if s:
                        act.wait_ge(sq_ready, 2 * t + 1)
                    A(spare[:, t, 2], rows_bank[:, 0:D], ACT.Square, scale=float(D) ** -0.5,
                      accum_out=mean_sq[:, t, s:s + 1]).then_inc(sq_ready, 1)

            def scale_v(t):
                act.wait_ge(v_rows_done, t + 1)
                act.wait_ge(root_ready[t], 2)
                A(spare[:, t, 3], v_bank[t][:, 0:D], ACT.Copy, scale=root[:, t, 0:1]).then_inc(v_rows_ready, 1)

            def norm_k(t):
                act.wait_ge(root_ready[t], 4)
                A(spare[:, t, 1], k_bank[t][:, 0:D], ACT.Copy, scale=root[:, t, 2:3]).then_inc(kn_ready, 1)

            def keep_q(t):
                act.wait_ge(qT_done, t + 1)
                act.wait_ge(lnw_ready, 1)
                for c in range(DC):
                    A(qT[:, t, c], qT_bank[t][:, c * P:(c + 1) * P], ACT.Copy,
                      scale=lnw_sb[:, c:c + 1]).then_inc(qT_ready, 1)

            def self_exp(t, h):
                act.wait_ge(a_shifted, 2 * t + h + 1)
                A(wide_a[:, 2 * t + h], wide_a[:, 2 * t + h], ACT.Exp, scale=ASCALE).then_inc(a_exp, 1)

            def keep_a(t, h):
                act.wait_ge(at_done, 2 * t + h + 1)
                A(wide_b[:, 2 * t + h], at_bank[t][h], ACT.Copy).then_inc(at_ready, 1)

            def keep_yn(t):
                keep_cols(t, yn_bank[t], ynT_done, ynT_ready)

            def keep_x2(t):
                keep_cols(t, x2_bank[t], x2T_done, x2T_ready)

            exps(0)
            for n in range(NC):
                high_p(n)
                exps(n + 1)
            for k in range(NC):
                high_p(NC + k)
                if k == 4:
                    keep_x1(0)
                if k == 5:
                    squares(0)
                if k == 7:
                    keep_q(0)
                if k + 1 < NC:
                    exps(NC + k + 1)
                if k == 2:
                    keep_an(0)
                if k == 5:
                    scale_v(0)
                    norm_k(0)
                if k == 7:
                    self_exp(0, 0)
                    self_exp(0, 1)
                    keep_a(0, 0)
                    keep_a(0, 1)
            keep_an(1)
            keep_x1(1)
            keep_yn(0)
            squares(1)
            norm_k(1)
            scale_v(1)
            keep_q(1)
            self_exp(1, 0)
            keep_x2(0)
            self_exp(1, 1)
            keep_a(1, 0)
            keep_a(1, 1)
            keep_yn(1)
            A(table_junk[:], warm_bf[:, 0:1], ACT.Gelu).then_inc(act_order, 1)
            keep_x2(1)
            for n in range(EGN * FH):
                act.wait_ge(f1_biased, n + 1)
                A(wide_a[:, n], wide_a[:, n], ACT.Gelu).then_inc(gelu_ready, 1)
            for t in range(TT):
                act.wait_ge(fin_done, t + 1)
                A(rows[:, t], fin_bank[t][:, 0:D], ACT.Gelu).then_inc(fin_gelu, 1)

        @block.vector
        def _(dve):
            V = nc.vector
            steps = [0]

            def counted(ins):
                steps[0] += 1
                ins.then_inc(dve_order, 1)
                return steps[0]

            def chain(ins):
                dve.wait_ge(dve_order, counted(ins))

            def variance(t, src):
                chain(V.bn_stats(bn6[:, t], src))
                chain(V.bn_aggr(mv[:, t], bn6[:, t]))

            V.memset(warm_bf[:], 0.0).then_inc(warm_ready, 1)
            V.memset(mean_of[:], 1.0 / D).then_inc(warm_ready, 1)
            V.memset(ones_row[:], 1.0).then_inc(warm_ready, 1)
            chain(V.memset(ones_col[:], 1.0))
            dve.wait_ge(ld_x, 16)
            for t in range(TT):
                variance(t, x_sb[:, t])
                V.tensor_scalar(base[:, t, 0:1], mv[:, t, 1:2], LN_EPS, None, ALU.add).then_inc(var_ready[t], 1)
            for t in range(TT):
                dve.wait_ge(root_ready[t], 1)
                V.tensor_scalar(xn[:, t], x_sb[:, t], mv[:, t, 0:1], root[:, t, 0:1], ALU.subtract,
                                ALU.mult).then_inc(xn_ready, 1)
            for t in range(TT):
                dve.wait_ge(xnT_done, t + 1)
                V.tensor_copy(xnT[:, :, t * P:(t + 1) * P],
                              bank[6 + t][:, 0:D].rearrange("p (c i) -> p c i", c=DC)).then_inc(xnT_ready, 1)

            def low_ctx(k):
                for c in range(DC):
                    dve.wait_ge(tH_ready, DC * k + c + 1)
                    V.tensor_tensor(tL[:, k % T_RING, c], bank[c], tH[:, k % T_RING, c].bitcast(F32),
                                    ALU.subtract).then_inc(tL_ready, 1)

            low_ctx(0)
            dve.wait_ge(ld_bq, 16)
            for e in range(DC):
                dve.wait_ge(q_done, e + 1)
                V.tensor_scalar(xqT[:, e], bank[2 + e][:, 0:TOK], bq_sb[:, e:e + 1], None, ALU.add).then_inc(q_ready, 1)
            for d in range(DC):
                dve.wait_ge(gH_ready, d + 1)
                V.tensor_tensor(gL[:, d], bank[4 + d][:, 0:TOK], gH[:, d].bitcast(F32), ALU.subtract).then_inc(gL_ready, 1)
            low_ctx(1)
            V.tensor_copy(cH[:, :, :, D:D + 2], ones_col[:].unsqueeze(2).unsqueeze(3).to_broadcast([P, NC, JB, 2])
                          ).then_inc(ones_col_ready, 1)

            def factors():
                dve.wait_ge(consts, 9)
                dve.wait_ge(ld_small, 16 * N_SMALL)
                chain(V.tensor_reduce(parity[:, 0:1], strip_even[:], AX.X, ALU.add))
                chain(V.tensor_scalar(parity[:, 1:2], parity[:, 0:1], -1.0, 1.0, ALU.mult, ALU.add))
                for par in range(2):
                    V.tensor_scalar(lnw_par[:, :, par], lnw_sb[:], parity[:, par:par + 1], None,
                                    ALU.mult).then_inc(lnw_ready, 1)
                V.tensor_copy(ident_bf[:], ident[:]).then_inc(idbf_ready, 1)
                for g in range(GT):
                    V.tensor_copy(shifted[:, g].rearrange("p (r i) -> p r i", r=2),
                                  ident[:, g * LS:(g + 1) * LS].unsqueeze(1).to_broadcast([P, 2, LS])
                                  ).then_inc(shifted_ready, 1)

            def scale_attnw():
                dve.wait_ge(attn_bias_done, 1)
                V.tensor_tensor(attnb_sb[:], bank[6][:, 0:DC], attnb_sb[:], ALU.add).then_inc(attnw_scaled, 1)
                for c in range(DC):
                    V.tensor_scalar(attnw_sb[:, c], attnw_sb[:, c], lng_sb[:, c:c + 1], None,
                                    ALU.mult).then_inc(attnw_scaled, 1)

            for k in range(NC):
                if 1 <= k < NC - 1:
                    low_ctx(k + 1)
                for h in range(2):
                    for t in range(TT):
                        n = TT * (2 * k + h) + t
                        dve.wait_ge(s_ready, n + 1)
                        blocks = scores[t][:, k].rearrange("p (b i) -> p b i", b=JB)[:, 2 * h:2 * h + 2]
                        if n < TT:
                            V.tensor_copy(top[:, t], blocks).then_inc(top_ready, 1)
                        else:
                            dve.wait_ge(top_ready, n - TT + 1)
                            V.tensor_tensor(top[:, t], top[:, t], blocks, ALU.max).then_inc(top_ready, 1)
                if k == 3:
                    dve.wait_ge(xbv_ready, TT)
                    dve.wait_ge(qbk_done, 1)
                    chain(V.tensor_copy(bias_row[:], bank[7][:, 0:TOK]))
                if k == 4:
                    scale_attnw()
                if k == 5:
                    factors()
            for t in range(TT):
                dve.wait_ge(topT_done, t + 1)
                V.tensor_reduce(row_max[:, t:t + 1], bank[t][:, 0:2 * P], AX.X, ALU.max).then_inc(row_max_ready, 1)

            def shift_rows(t):
                dve.wait_ge(max_row_done, t + 1)
                bias = bias_row[:, t * P:(t + 1) * P]
                chain(V.tensor_tensor(shift_row[:, t], bank[4 + t][:, 0:P], bias, ALU.add))
                V.tensor_tensor(shift_row[:, t], bias, shift_row[:, t], ALU.subtract).then_inc(shift_row_ready, 1)

            def shift(n):
                t, k = divmod(n, NC)
                dve.wait_ge(shift_row_ready, t + 1)
                blocks = scores[t][:, k].rearrange("p (b i) -> p b i", b=JB)
                V.tensor_tensor(blocks, blocks, shift_row[:, t].unsqueeze(1).to_broadcast([P, JB, P]),
                                ALU.add).then_inc(s_shifted, 1)

            def low_p(n):
                dve.wait_ge(pH_ready, n + 1)
                V.tensor_tensor(pL[:, n % P_RING], scores[0][:, n], pH[:, n % P_RING].bitcast(F32),
                                ALU.subtract).then_inc(pL_first_ready, 1)

            shift_rows(0)
            shift(0)
            shift(1)
            low_p(0)
            shift(2)
            low_p(1)
            shift(3)
            shift_rows(1)

            def centre_qkv(c):
                dve.wait_ge(qkv_mean_done, 1)
                V.tensor_tensor(wqkv_sb[:, c, 0:2 * D], wqkv_sb[:, c, 0:2 * D], bank[2],
                                ALU.subtract).then_inc(qkv_centred, 1)
                V.tensor_tensor(wqkv_sb[:, c, 2 * D:3 * D], wqkv_sb[:, c, 2 * D:3 * D], bank[3][:, 0:D],
                                ALU.subtract).then_inc(qkv_centred, 1)

            def centre_attnw():
                dve.wait_ge(attnw_mean_done, 1)
                dve.wait_ge(attnw_scaled, DC + 1)
                for c in range(DC):
                    V.tensor_tensor(attnw_sb[:, c], attnw_sb[:, c], bank[7][:, 0:D],
                                    ALU.subtract).then_inc(attnw_centred, 1)

            def divide_an(t):
                dve.wait_ge(pv_done, NC * (t + 1))
                chain(V.reciprocal(inv_sum[:, t:t + 1], A_bank[t][:, D:D + 1]))
                V.tensor_scalar(rows[:, t], A_bank[t][:, 0:D], inv_sum[:, t:t + 1], None, ALU.mult).then_inc(an_ready, 1)

            def add_xattn(t):
                dve.wait_ge(xo_done, t + 1)
                dve.wait_ge(xbv_ready, TT)
                V.tensor_tensor(x_sb[:, t], xo_bank[t][:, 0:D], xres[:, t], ALU.add).then_inc(x1_ready, 1)
                dve.wait_ge(x1_ready, t + 1)
                variance(t, x_sb[:, t])
                V.tensor_scalar(base[:, t, 0:1], mv[:, t, 1:2], LN_EPS, None, ALU.add).then_inc(var_ready[t], 1)
                chain(V.tensor_scalar(rms_eps[:, t:t + 1], mv[:, t, 1:2], RMS_EPS, RMS_EPS * LN_EPS, ALU.mult, ALU.add))

            def add_rms_eps(t, s):
                dve.wait_ge(sq_ready, 2 * t + s + 1)
                V.tensor_scalar(base[:, t, 1 + s:2 + s], mean_sq[:, t, s:s + 1], rms_eps[:, t:t + 1], None,
                                ALU.add).then_inc(var_ready[t], 1)

            def norm_q(t):
                dve.wait_ge(root_ready[t], 3)
                V.tensor_scalar(spare[:, t, 0], q_bank[t][:, 0:D], root[:, t, 1:2], None, ALU.mult).then_inc(qn_ready, 1)

            def keep_v(t):
                dve.wait_ge(v_done, t + 1)
                dve.wait_ge(ones_ready, 3)
                for par in range(2):
                    half = slice(par * LS, (par + 1) * LS)
                    src = v_bank[t][half, :].rearrange("p (g n r e) -> p g n r e", g=GT, r=2, e=HD)[:, :, :, par]
                    V.tensor_copy(v2[half, t, :, :, par, 0:HD], src).then_inc(v_ready, 1)

            def keep_k(t):
                dve.wait_ge(kT_done, t + 1)
                dve.wait_ge(lnw_ready, 2)
                src = kT_bank[t][:, 0:DC * P].rearrange("p (c i) -> p c i", c=DC)
                for c in range(DC):
                    ins = V.tensor_tensor(kT[:, t, c], src[:, c].unsqueeze(1).to_broadcast([P, 2, P]),
                                          lnw_par[:, c].unsqueeze(2).to_broadcast([P, 2, P]), ALU.mult)
                ins.then_inc(kT_ready, 1)

            def shift_scores(t, h):
                dve.wait_ge(a_done, 2 * t + h + 1)
                first = a_first[t] + 2 * h
                strips = psum[:, first:first + 2, 0:4 * LS].rearrange("p i (a k) -> p i a k", k=LS)
                V.tensor_reduce(head_max[:, t, 2 * h:2 * h + 2], strips, AX.X, ALU.max).then_inc(a_max, 1)
                dve.wait_ge(a_max, 2 * t + h + 1)
                dst = wide_a[:, 2 * t + h].rearrange("p (i a k) -> p i a k", i=2, k=LS)
                for i in range(2):
                    ins = V.tensor_tensor(dst[:, i], strips[:, i],
                                          head_max[:, t, 2 * h + i].unsqueeze(2).to_broadcast([P, 4, LS]), ALU.subtract)
                ins.then_inc(a_shifted, 1)

            def divide_y(t):
                dve.wait_ge(y_done, t + 1)
                y = y_bank[t][:, 0:HEADS * VW].rearrange("p (n e) -> p n e", e=VW)
                chain(V.reciprocal(inv_den[:, t], y[:, :, HD]))
                V.tensor_tensor(rows[:, t].rearrange("p (n e) -> p n e", e=HD), y[:, :, 0:HD],
                                inv_den[:, t].unsqueeze(2).to_broadcast([P, HEADS, HD]), ALU.mult).then_inc(yn_ready, 1)

            def add_self(t):
                dve.wait_ge(proj_done, t + 1)
                V.tensor_tensor(xres[:, t], proj_bank[t][:, 0:D], x_sb[:, t], ALU.add).then_inc(x2_ready, 1)
                dve.wait_ge(x2_ready, t + 1)
                variance(t, xres[:, t])
                V.tensor_scalar(base[:, t, 3:4], mv[:, t, 1:2], LN_EPS, None, ALU.add).then_inc(var_ready[t], 1)
                V.tensor_scalar(base[:, t, 4:5], mv[:, t, 1:2], 1.0 + LN_EPS, LN_EPS * LN_EPS, ALU.mult,
                                ALU.add).then_inc(var_ready[t], 1)

            def norm_h0(t):
                dve.wait_ge(root_ready[t], 5)
                chain(V.tensor_scalar(h0[:, t], xres[:, t], mv[:, t, 0:1], root[:, t, 3:4], ALU.subtract, ALU.mult))

            def add_h0(t):
                dve.wait_ge(root_ready[t], 6)
                dve.wait_ge(xa_done, t + 1)
                V.scalar_tensor_tensor(rows[:, t], xa_bank[t][:, 0:D], root[:, t, 4:5], h0[:, t], ALU.mult,
                                       ALU.add).then_inc(xa_rows_ready, 1)

            def keep_xa(t):
                dve.wait_ge(xaT_done, t + 1)
                V.tensor_tensor(xaT[:].rearrange("p c (e m i) -> p c e m i", m=MICRO, i=TPE)[:, :, :, t],
                                xaT_bank[t][:, 0:D].rearrange("p (c e i) -> p c e i", c=DC, i=TPE),
                                attnb_sb[:].unsqueeze(2).unsqueeze(3).to_broadcast([P, DC, E, TPE]),
                                ALU.add).then_inc(xaT_ready, 1)

            for n in range(4, NC + 2):
                shift(n)
                if n == 6:
                    centre_attnw()
                if n > NC - 1:
                    centre_qkv(n - NC)
            for k in range(NC):
                if k + 2 < NC:
                    shift(NC + k + 2)
                if k == 1:
                    divide_an(0)
                if k == 3:
                    add_xattn(0)
                if k == 6:
                    add_rms_eps(0, 0)
                    add_rms_eps(0, 1)
                    norm_q(0)
                if k == 7:
                    keep_k(0)
                    shift_scores(0, 0)
                    shift_scores(0, 1)
                    keep_v(0)
            divide_an(1)
            divide_y(0)
            add_xattn(1)
            add_rms_eps(1, 0)
            add_rms_eps(1, 1)
            norm_q(1)
            keep_k(1)
            add_self(0)
            shift_scores(1, 0)
            shift_scores(1, 1)
            norm_h0(0)
            keep_v(1)
            add_h0(0)
            divide_y(1)
            add_self(1)
            keep_xa(0)
            norm_h0(1)
            add_h0(1)
            keep_xa(1)

            def bias1(n):
                dve.wait_ge(f1_done, n + 1)
                V.tensor_tensor(wide_a[:, n], f1_bank[n], b1_sb[:, n // FH, (n % FH) * HALF:(n % FH + 1) * HALF],
                                ALU.add).then_inc(f1_biased, 1)

            def keep_h(n):
                dve.wait_ge(hT_done, n + 1)
                V.tensor_copy(wide_b[:, n], hT_bank[n]).then_inc(hT_ready, 1)

            def bias2(g):
                dve.wait_ge(f2_done, g + 1)
                V.tensor_tensor(h0[:, g], f2_bank[g][:, 0:D], b2_sb[:, g], ALU.add).then_inc(f2_ready, 1)

            def keep_y(g):
                dve.wait_ge(yT_done, g + 1)
                for m in range(MICRO):
                    dst = qT[:, m].rearrange("p c (e i) -> p c e i", i=TPE)[:, :, g * EG:(g + 1) * EG]
                    src = yT_bank[g][:, 0:D].rearrange("p (c e m i) -> p c e m i", c=DC, m=MICRO, i=TPE)
                    V.tensor_copy(dst, src[:, :, :, m]).then_inc(yT_ready, 1)

            dve.wait_ge(ld_late, 16 * N_LATE)
            bias1(0)
            bias1(1)
            keep_h(0)
            bias1(2)
            keep_h(1)
            bias1(3)
            keep_h(2)
            keep_h(3)
            bias2(0)
            keep_y(0)
            bias2(1)
            keep_y(1)
            for t in range(TT):
                dve.wait_ge(fin_gelu, t + 1)
                V.tensor_tensor(xres[:, t], xres[:, t], rows[:, t], ALU.add).then_inc(out_ready, 1)


_INS = ["x", "ctx_1024", "L0_xattn_Wq", "L0_xattn_bq", "L0_xattn_Wk", "L0_xattn_bk", "L0_xattn_Wv", "L0_xattn_bv",
        "L0_attn_w_qkv", "L0_attn_ln_w", "L0_attn_w_proj", "L0_ffn_ln_g", "L0_ffn_ln_b", "L0_ffn_attn_w",
        "L0_ffn_attn_b", "L0_ffn_w1", "L0_ffn_b1", "L0_ffn_w2", "L0_ffn_b2", "L0_ffn_next_w", "L0_ffn_next_b"]


def kernel(**inputs):
    import numpy as _np
    import concourse.bacc as _bacc
    from concourse import mybir as _mybir
    from concourse.bass_utils import run_bass_kernel_spmd as _run

    nc = _bacc.Bacc("TRN2", target_bir_lowering=False, num_devices=1)
    arrays, args = {}, []
    for name in _INS:
        a = _np.ascontiguousarray(inputs[name])
        arrays[f"in_{name}"] = a
        args.append(nc.dram_tensor(f"in_{name}", a.shape, _mybir.dt.from_np(a.dtype), kind="ExternalInput").ap())
    args.append(nc.dram_tensor("out_x", (1, 256, 256), _mybir.dt.float32, kind="ExternalOutput").ap())
    perceiver_block(nc, *args)
    r = _run(nc, [arrays], core_ids=[0])
    return r.results[0]["out_x"]
```
